# Optimizing a Trainium2 kernel written in Bass

```python
import numpy as np
import jax
import jax.numpy as jnp

def _softmax(x, axis=-1):
    return jax.nn.softmax(x, axis=axis)

def _gelu(x):
    return jax.nn.gelu(x, approximate=True)

def _silu(x):
    return jax.nn.silu(x)

def _sigmoid(x):
    return jax.nn.sigmoid(x)

def _layernorm(x, axis=-1, eps=1e-05):
    m = jnp.mean(x, axis=axis, keepdims=True)
    v = jnp.var(x, axis=axis, keepdims=True)
    return (x - m) / jnp.sqrt(v + eps)

def _scatter_add(tgt, idx, src, axis=0):
    return tgt.at[idx].add(src)

def _segment_sum(src, seg, n):
    return jax.ops.segment_sum(src, seg, n)
kernel_name = 'mk_adaln_d2_jaxref_r8_11a483'

def setup_inputs(seed: int=0):
    np.random.seed(seed)
    _w = jnp.asarray

    def _L0_attn_setup():
        import jax, jax.numpy as jnp
        import numpy as np
        NEG_FILL = jnp.finfo(jnp.float32).min
        key = jax.random.key(seed)
        k0, k1, k2, k3, k4 = jax.random.split(key, 5)
        B, N, E, D = (4, 512, 128, 32)
        STD = 0.05
        inputs = jax.random.normal(k0, (B, N, E), dtype=jnp.float32)
        Wq = STD * jax.random.normal(k1, (E, D), dtype=jnp.float32)
        Wk = STD * jax.random.normal(k2, (E, D), dtype=jnp.float32)
        Wvdown = STD * jax.random.normal(k3, (E, D), dtype=jnp.float32)
        Wvup = STD * jax.random.normal(k4, (D, E), dtype=jnp.float32)
        return {'inputs': inputs, 'Wq': Wq, 'Wk': Wk, 'Wvdown': Wvdown, 'Wvup': Wvup}
    _L0_attn_in = _L0_attn_setup()

    def _L0_ffn_setup():
        import jax, jax.numpy as jnp
        import numpy as np
        B, S, D, E = (4, 512, 128, 8)
        key = jax.random.key(seed)
        k1, k2, k3, k4, k5 = jax.random.split(key, 5)
        scale = 1.0 / np.sqrt(D)
        return {'x': jax.random.normal(k1, (B, S, D), dtype=jnp.float32), 'Wg': jax.random.normal(k2, (D, D), dtype=jnp.float32) * scale, 'bg': jnp.zeros((D,), dtype=jnp.float32), 'We': jax.random.normal(k3, (E, D, D), dtype=jnp.float32) * scale, 'be': jnp.zeros((E, D), dtype=jnp.float32)}
    _L0_ffn_in = _L0_ffn_setup()
    _L0_c = _w((lambda *s: np.random.randn(*s).astype(np.float32) * 0.05)(8, 128))
    _L0_wmod = _w((lambda *s: np.random.randn(*s).astype(np.float32) * 0.05)(128, 6 * 128) * 128 ** (-0.5))

    def _L1_attn_setup():
        import jax, jax.numpy as jnp
        import numpy as np
        HEADS = 16
        key = jax.random.key(seed)
        ks = jax.random.split(key, 6)
        b, n, c = (4, 256, 128)
        h = 128
        s = 0.02
        return {'x': jax.random.normal(ks[0], (b, n, c), jnp.float32), 'Wq': jax.random.normal(ks[1], (h, c), jnp.float32) * s, 'Wk': jax.random.normal(ks[2], (h, c), jnp.float32) * s, 'Wv': jax.random.normal(ks[3], (h, c), jnp.float32) * s, 'Wout': jax.random.normal(ks[4], (c, h), jnp.float32) * s, 'bout': jnp.zeros((c,), jnp.float32)}
    _L1_attn_in = _L1_attn_setup()

    def _L1_ffn_setup():
        import jax, jax.numpy as jnp
        import numpy as np
        NUM_GEMMS = 8
        HIDDEN = 128
        INTER = 512
        key = jax.random.key(seed)
        k_x, k_w1, k_b1, k_w2, k_b2 = jax.random.split(key, 5)
        x = jax.random.normal(k_x, (8, 256, HIDDEN), dtype=jnp.float32)
        s1 = 1.0 / np.sqrt(HIDDEN)
        s2 = 1.0 / np.sqrt(INTER)
        W1 = jax.random.uniform(k_w1, (NUM_GEMMS, INTER, HIDDEN), jnp.float32, -s1, s1)
        b1 = jax.random.uniform(k_b1, (NUM_GEMMS, INTER), jnp.float32, -s1, s1)
        W2 = jax.random.uniform(k_w2, (NUM_GEMMS, HIDDEN, INTER), jnp.float32, -s2, s2)
        b2 = jax.random.uniform(k_b2, (NUM_GEMMS, HIDDEN), jnp.float32, -s2, s2)
        return {'x': x, 'W1': W1, 'b1': b1, 'W2': W2, 'b2': b2}
    _L1_ffn_in = _L1_ffn_setup()
    _L1_c = _w((lambda *s: np.random.randn(*s).astype(np.float32) * 0.05)(8, 128))
    _L1_wmod = _w((lambda *s: np.random.randn(*s).astype(np.float32) * 0.05)(128, 6 * 128) * 128 ** (-0.5))
    _d = {'L0_attn_inputs': _L0_attn_in['inputs'], 'L0_attn_Wq': _L0_attn_in['Wq'], 'L0_attn_Wk': _L0_attn_in['Wk'], 'L0_attn_Wvdown': _L0_attn_in['Wvdown'], 'L0_attn_Wvup': _L0_attn_in['Wvup'], 'L0_ffn_Wg': _L0_ffn_in['Wg'], 'L0_ffn_bg': _L0_ffn_in['bg'], 'L0_ffn_We': _L0_ffn_in['We'], 'L0_ffn_be': _L0_ffn_in['be'], 'L0_c': _L0_c, 'L0_wmod': _L0_wmod, 'L1_attn_Wq': _L1_attn_in['Wq'], 'L1_attn_Wk': _L1_attn_in['Wk'], 'L1_attn_Wv': _L1_attn_in['Wv'], 'L1_attn_Wout': _L1_attn_in['Wout'], 'L1_attn_bout': _L1_attn_in['bout'], 'L1_ffn_W1': _L1_ffn_in['W1'], 'L1_ffn_b1': _L1_ffn_in['b1'], 'L1_ffn_W2': _L1_ffn_in['W2'], 'L1_ffn_b2': _L1_ffn_in['b2'], 'L1_c': _L1_c, 'L1_wmod': _L1_wmod}
    _x0 = _d['L0_attn_inputs']
    _d['L0_attn_inputs'] = jax.random.normal(jax.random.fold_in(jax.random.key(seed), 1), (8, 1024, 128), dtype=_x0.dtype)
    del _x0
    return _d

def reference(L0_attn_inputs, L0_attn_Wq, L0_attn_Wk, L0_attn_Wvdown, L0_attn_Wvup, L0_ffn_Wg, L0_ffn_bg, L0_ffn_We, L0_ffn_be, L0_c, L0_wmod, L1_attn_Wq, L1_attn_Wk, L1_attn_Wv, L1_attn_Wout, L1_attn_bout, L1_ffn_W1, L1_ffn_b1, L1_ffn_W2, L1_ffn_b2, L1_c, L1_wmod):

    def _L0_attn_ref(inputs, Wq, Wk, Wvdown, Wvup):
        import jax, jax.numpy as jnp
        import numpy as np
        NEG_FILL = jnp.finfo(jnp.float32).min
        B, N, E = inputs.shape
        D = Wq.shape[1]
        Q = inputs @ Wq
        K = inputs @ Wk
        score = jnp.einsum('bqd,bkd->bqk', Q, K)
        score = score / jnp.sqrt(jnp.float32(D))
        causal = jnp.tril(jnp.ones((N, N), dtype=bool))
        score = jnp.where(causal, score, 0.0)
        score = jnp.where(score != 0, score, NEG_FILL)
        attn = jax.nn.softmax(score, axis=-1)
        V = inputs @ (Wvdown @ Wvup)
        return attn @ V

    def _L0_ffn_ref(x, Wg, bg, We, be):
        import jax, jax.numpy as jnp
        import numpy as np
        B, S, D, E = (4, 512, 128, 8)
        probs = jax.nn.softmax(x @ Wg + bg, axis=-1)
        idx = jnp.argmax(probs, axis=-1)
        p = jnp.take_along_axis(probs, idx[..., None], axis=-1)[..., 0]
        e_idx = idx % We.shape[0]
        h = jax.nn.relu(jnp.einsum('bsd,edf->besf', x, We) + be[None, :, None, :])
        onehot = jax.nn.one_hot(e_idx, We.shape[0], dtype=x.dtype)
        out = jnp.einsum('besf,bse->bsf', h, onehot) * p[..., None]
        return out

    def _L1_attn_ref(x, Wq, Wk, Wv, Wout, bout):
        import jax, jax.numpy as jnp
        import numpy as np
        HEADS = 16
        b, n, c = x.shape
        m = HEADS
        d = Wq.shape[0] // m
        q = jnp.einsum('bnc,hc->bnh', x, Wq).reshape(b, n, m, d)
        k = jnp.einsum('bnc,hc->bnh', x, Wk).reshape(b, n, m, d)
        v = jnp.einsum('bnc,hc->bnh', x, Wv).reshape(b, n, m, d)
        scale = d ** (-0.25)
        weight = jnp.einsum('bimd,bjmd->bmij', q * scale, k * scale)
        weight = jax.nn.softmax(weight, axis=-1)
        a = jnp.einsum('bmij,bjmd->bimd', weight, v).reshape(b, n, m * d)
        return jnp.einsum('bnh,ch->bnc', a, Wout) + bout

    def _L1_ffn_ref(x, W1, b1, W2, b2):
        import jax, jax.numpy as jnp
        import numpy as np
        NUM_GEMMS = 8
        HIDDEN = 128
        INTER = 512
        orig_shape = x.shape
        token_num = int(np.prod(orig_shape[:-1]))
        m = token_num // NUM_GEMMS
        xg = x.reshape(NUM_GEMMS, m, HIDDEN)
        h1 = jnp.einsum('gmh,goh->gmo', xg, W1) + b1[:, None, :]
        h2 = jnp.einsum('gmo,gho->gmh', h1, W2) + b2[:, None, :]
        return h2.reshape(orig_shape)
    x = L0_attn_inputs
    mod = (_silu(L0_c) @ L0_wmod).reshape(L0_c.shape[0], 6, 1, -1)
    sa, ca, ga, sb, cb, gb = (mod[:, 0], mod[:, 1], mod[:, 2], mod[:, 3], mod[:, 4], mod[:, 5])
    ga = (2 * (ga >= 0) - 1) * jnp.maximum(jnp.abs(ga), 0.25)
    gb = (2 * (gb >= 0) - 1) * jnp.maximum(jnp.abs(gb), 0.25)
    h = _layernorm(x, axis=-1) * (1 + ca) + sa
    x = x + ga * _L0_attn_ref(h, L0_attn_Wq, L0_attn_Wk, L0_attn_Wvdown, L0_attn_Wvup)
    h = _layernorm(x, axis=-1) * (1 + cb) + sb
    x = x + gb * _L0_ffn_ref(h, L0_ffn_Wg, L0_ffn_bg, L0_ffn_We, L0_ffn_be)
    mod = (_silu(L1_c) @ L1_wmod).reshape(L1_c.shape[0], 6, 1, -1)
    sa, ca, ga, sb, cb, gb = (mod[:, 0], mod[:, 1], mod[:, 2], mod[:, 3], mod[:, 4], mod[:, 5])
    ga = (2 * (ga >= 0) - 1) * jnp.maximum(jnp.abs(ga), 0.25)
    gb = (2 * (gb >= 0) - 1) * jnp.maximum(jnp.abs(gb), 0.25)
    h = _layernorm(x, axis=-1) * (1 + ca) + sa
    x = x + ga * _L1_attn_ref(h, L1_attn_Wq, L1_attn_Wk, L1_attn_Wv, L1_attn_Wout, L1_attn_bout)
    h = _layernorm(x, axis=-1) * (1 + cb) + sb
    x = x + gb * _L1_ffn_ref(h, L1_ffn_W1, L1_ffn_b1, L1_ffn_W2, L1_ffn_b2)
    return x

_drawn_inputs = setup_inputs


def setup_inputs(seed=0):
    import zlib

    import numpy as np

    out = dict(_drawn_inputs(seed))
    spreads = {'L0_ffn_bg': (0.0, 0.8), 'L0_ffn_be': (0.0, 0.8), 'L1_attn_bout': (0.0, 0.291)}
    factors = {'L0_attn_Wq': 8.0,
     'L0_attn_Wk': 8.0,
     'L0_attn_Wvdown': 8.0,
     'L0_attn_Wvup': 8.0,
     'L0_ffn_Wg': 5.147,
     'L0_ffn_We': 5.209,
     'L0_c': 4.17,
     'L0_wmod': 4.045,
     'L1_attn_Wq': 8.0,
     'L1_attn_Wk': 8.0,
     'L1_attn_Wv': 8.0,
     'L1_attn_Wout': 8.0,
     'L1_ffn_b1': 7.949,
     'L1_ffn_b2': 24.225}
    for name, (base, spread) in spreads.items():
        noise = np.random.default_rng([zlib.crc32(name.encode()), seed]).standard_normal(out[name].shape)
        drawn = base * np.exp(spread * noise) if base else spread * noise
        out[name] = jnp.asarray(drawn.astype(out[name].dtype))
    for name, factor in factors.items():
        out[name] = (out[name] * factor).astype(out[name].dtype)
    return out
```

```python
import numpy as np
import concourse.bass as bass
import concourse.mybir as mybir

F32 = mybir.dt.float32
BF16 = mybir.dt.bfloat16
U32 = mybir.dt.uint32
ALU = mybir.AluOpType
ACT = mybir.ActivationFunctionType
AX = mybir.AxisListType

P = 128
B, N, C = 8, 1024, 128
T = N // P
D0 = 32
EXPERTS = 8
HEADS, DH = 16, 8
INTER = 512
KC = INTER // P
BANK = 512
HALVES = N // BANK
EPS = 1e-5
NEG = float(np.finfo(np.float32).min)
PARTS = 3
Q_PART = (0, 0, 0, 1, 1, 2)
K_PART = (0, 1, 2, 0, 1, 0)
K_MAX = 96
K_EXP = K_MAX + PARTS
GROUP = 4
GROUPS = HEADS // GROUP
SLOTS = 3
VW = 16
LEAD = 3


class Semaphores:

    def __init__(self, nc, ctx):
        self.nc, self.ctx, self.made, self.value = nc, ctx, {}, {}

    def mark(self, name, by):
        if name not in self.made:
            self.made[name] = self.ctx.enter_context(self.nc.semaphore(name))
            self.value[name] = 0
        self.value[name] += by
        return name, self.value[name]


class Queue:

    def __init__(self, engine, sems):
        self.engine, self.sems, self.reached = engine, sems, {}

    def wait(self, *marks):
        for m in marks:
            if m is not None and self.reached.get(m[0], 0) < m[1]:
                self.reached[m[0]] = m[1]
                self.engine.wait_ge(self.sems.made[m[0]], m[1])

    def raises(self, instruction, signal, by):
        if signal is None:
            return None
        m = self.sems.mark(signal, by)
        instruction.then_inc(self.sems.made[signal], by)
        return m

    def do(self, issue, signal=None):
        return self.raises(issue(self.engine), signal, 1)

    def dma(self, out, in_, signal):
        return self.raises(self.engine.dma_start(out, in_), signal, 16)


class Bank:

    def __init__(self, view):
        self.view, self.free = view, None


class Ring:
    def __init__(self, banks):
        self.banks, self.at = banks, 0

    def take(self):
        self.at += 1
        return self.banks[(self.at - 1) % len(self.banks)]


def build(nc, ctx, x_in, Wq0, Wk0, Wvdown, Wvup, Wg, bg, We, be, c0, wmod0,
          Wq1, Wk1, Wv1, Wout, bout, W1, b1, W2, b2, c1, wmod1, consts, select, out):
    sems = Semaphores(nc, ctx)
    pe, act, dve, pool, sp = (Queue(e, sems) for e in (nc.tensor, nc.scalar, nc.vector, nc.gpsimd, nc.sync))

    def sb(name, shape, dt=F32):
        return ctx.enter_context(nc.sbuf_tensor(name, shape, dt))

    score_psum = [ctx.enter_context(nc.psum_tensor(f"scores{i}", [P, N], F32)) for i in range(2)]
    pv_psum = ctx.enter_context(nc.psum_tensor("pv", [P, BANK], F32))
    ring_psum = [ctx.enter_context(nc.psum_tensor(f"ring{i}", [P, BANK], F32)) for i in range(3)]
    score_banks = [[Bank(score_psum[i][:, h * BANK:(h + 1) * BANK]) for h in range(HALVES)] for i in range(2)]
    pv_bank = Bank(pv_psum[:, :])
    ring_banks = [Bank(r[:, :]) for r in ring_psum]
    shared = Ring(ring_banks)
    wide = Ring(ring_banks + score_banks[0] + score_banks[1])
    ring = [wide]

    def take():
        bank = ring[0].take()
        pe.wait(bank.free)
        return bank

    const_sb = sb("consts", [P, 2 * P + EXPERTS])
    ident, tril, iota8 = const_sb[:, 0:P], const_sb[:, P:2 * P], const_sb[:, 2 * P:]
    ident_bf = sb("ident_bf", [P, P], BF16)
    sel = sb("select", [B, B, P])
    minus_half = sb("minus_half", [P, T])

    wqk0 = sb("wqk0", [C, 2 * D0])
    wv0 = sb("wv0", [C, C])
    wg, we = sb("wg", [C, C]), sb("we", [C, EXPERTS, C])
    bg_rows, bout_rows = sb("bg_rows", [P, C]), sb("bout_rows", [P, C])
    be3 = sb("be3", [PARTS * EXPERTS, C], BF16)
    wT1 = sb("wT1", [P, 4, P])
    b1_nat, b1T, b2_sb = sb("b1_nat", [B * KC, P]), sb("b1T", [P, B * KC]), sb("b2_sb", [B, C])
    cT = sb("cT", [C, 2, B])
    modT = sb("modT", [C, 2, 4, B])
    gate_sb = sb("gate_sb", [B, 4, C])

    gates = [sb(f"gates{i}", [P, 4, C]) for i in range(3)]
    xs = [sb(f"x{i}", [P, T, C]) for i in range(4)]
    xn_f, hT_f = sb("xn_f", [P, T, C]), sb("hT_f", [C, N])
    st_f, mv_f, sm_f = sb("st_f", [P, T, 6]), sb("mv_f", [P, T, 2]), sb("sm_f", [P, 3, T])
    wv0b = sb("wv0b", [C, C])
    qk1_parts = [sb("q1_parts", [P, PARTS, N], BF16), sb("k1_parts", [P, PARTS, N], BF16)]
    qk0_parts = qk1_parts[0][0:2 * D0, :, :]
    rest = sb("rest", [P, N])
    q0_ops, k0_ops = qk1_parts[1][0:3 * D0, 0:2, :], sb("k0_ops", [3 * D0, 2, N], BF16)
    v0 = sb("v0", [P, T, C + 1])
    v0_later = sb("v0_later", [P, T - 1, C + 1])
    s0 = [sb(f"s0_{i}", [P, (T + 1) * P]) for i in range(2)]
    p0T = [sb("p0T", [P, T + 1, P])]
    nm0, rs0 = sb("nm0", [P, T]), sb("rs0", [P, T])
    mx0 = sb("mx0", [P, T])
    top8, idx8 = sb("top8", [P, T, 8]), sb("idx8", [P, T, 8], U32)
    eidx, eidx_f = sb("eidx", [P, T], U32), sb("eidx_f", [P, T])
    ngmx, gsum, gp = sb("ngmx", [P, T]), sb("gsum", [P, T]), sb("gp", [P, T])
    onehot = sb("onehot", [P, T, PARTS, EXPERTS], BF16)
    onehotT = sb("onehotT", [PARTS * EXPERTS, N], BF16)
    hm = sb("hm", [C, EXPERTS, P])
    q_ops = sb("q_ops", [P, SLOTS, GROUP, N], BF16)
    k_ops = sb("k_ops", [P, SLOTS, GROUP, N], BF16)
    v1 = [sb(f"v1_{i}", [P, T, HEADS, VW]) for i in range(2)]
    p_sb = [sb(f"p{i}", [P, N]) for i in range(4)]
    mx = [sb(f"row_max{i}", [P, GROUP * T, HALVES]) for i in range(2)]
    nm = sb("nm", [P, GROUP * T])
    nm_f, nm_r = sb("nm_f", [GROUP * T, P]), sb("nm_r", [GROUP * T, P])
    nm_parts = [sb(f"nm_parts{i}", [GROUP * T, PARTS, P], BF16) for i in range(2)]
    o_sb = sb("o_sb", [P, BANK])
    nd = sb("nd", [HEADS * DH, 2, N])
    xn_b = sb("xn_b", [P, T, C])
    hT_b = sb("hT_b", [C, N])
    st_b, mv_b, sm_b = sb("st_b", [P, T, 6]), sb("mv_b", [P, T, 2]), sb("sm_b", [P, 3, T])
    w1_sb, w2_sb = sb("w1_sb", [P, KC, C]), sb("w2_sb", [C, INTER])
    w2T = sb("w2T", [P, KC, C])
    wmod = [nd[:, j, 0:6 * C].rearrange("p (j c) -> p j c", c=C) for j in range(2)]
    w_nat = w1_sb
    gate_s = w2_sb[0:B, :].rearrange("p (j c) -> p j c", c=C)
    c_sb, c_e = (hT_b[0:B, i * 2 * C:(i + 1) * 2 * C].rearrange("p (l c) -> p l c", c=C) for i in range(2))
    wvd, wvu, wvdT = hT_b[:, 512:512 + D0], hT_b[0:D0, 640:640 + C], hT_b[0:D0, 768:768 + C]
    be_f, be_r = o_sb[0:EXPERTS, 0:C], o_sb[0:EXPERTS, C:2 * C]
    be_parts = o_sb[0:EXPERTS, 2 * C:2 * C + PARTS * C // 2].bitcast(BF16).rearrange("p (r c) -> p r c", c=C)
    wff = sb("wff", [C, 2, C])
    woutb, boutb = sb("woutb", [C, C]), sb("boutb", [P, C])
    parts_dram = nc.dram_tensor("parts", [2, 2, PARTS, P, N], BF16, kind="Internal").ap()

    def load(dst, src, signal="in_setup"):
        return sp.dma(dst, src, signal)

    x_loaded = {}

    def load_x(b, after=None):
        sp.wait(after)
        x_loaded[b] = sp.dma(xs[b % 4][:, :, :], x_in[b].rearrange("(t p) c -> p t c", p=P), f"in_x{b % 4}")

    load_x(0)
    for dst, src in ((const_sb[:, :], consts), (c_sb[:, 0, :], c0), (c_sb[:, 1, :], c1),
                     (wmod[0][:, :, :], wmod0.rearrange("k (j c) -> k j c", c=C)),
                     (wmod[1][:, :, :], wmod1.rearrange("k (j c) -> k j c", c=C)),
                     (wvd[:, :], Wvdown), (wvu[:, :], Wvup)):
        loaded = load(dst, src)
    loaded_first = loaded
    for dst, src in ((wqk0[:, 0:D0], Wq0), (wqk0[:, D0:], Wk0), (sel[:, :, :], select.rearrange("k (b p) -> k b p", p=P)),
                     (wg[:, :], Wg), (bg_rows[:, :], bg.partition_broadcast(P)),
                     (we[:, :, :], We.rearrange("e c f -> c e f")), (be_f[:, :], be),
                     (w_nat[:, 0, :], Wq1), (w_nat[:, 1, :], Wk1), (w_nat[:, 2, :], Wv1), (w_nat[:, 3, :], Wout),
                     (bout_rows[:, :], bout.partition_broadcast(P)),
                     (b1_nat[:, :], b1.rearrange("g (k o) -> (g k) o", o=P)), (b2_sb[:, :], b2)):
        loaded_rest = load(dst, src, "in_rest")
    load_x(1)

    k_zero = pool.do(lambda e: e.memset(k_ops[:, :, :, :].bitcast(F32), 0.0), "pool")
    mh_ready = dve.do(lambda e: e.memset(minus_half[:, :], -0.5), "dve")
    pv_bank.free = dve.do(lambda e: e.memset(pv_psum[:, :], 0.0), "dve")
    v0_ones = dve.do(lambda e: e.memset(v0[:, :, C:C + 1], 1.0), "dve")
    q_zero = dve.do(lambda e: e.memset(q_ops[:, :, :, :].bitcast(F32), 0.0), "dve")
    for v in v1:
        v1_ones = dve.do(lambda e, v=v: e.memset(v[:, :, :, DH:VW], 1.0), "dve")

    dve.wait(k_zero)
    k_ready = dve.do(lambda e: e.memset(k_ops[K_MAX:K_EXP, :, :, :], 1.0), "dve")

    act.wait(loaded_first)
    m = act.do(lambda e: e.activation(c_e[:, :, :], c_sb[:, :, :], ACT.Exp, scale=-1.0), "act")
    dve.wait(m)
    m = dve.do(lambda e: e.tensor_scalar(c_e[:, :, :], c_e[:, :, :], 1.0, None, ALU.add), "dve")
    dve.wait(m)
    m = dve.do(lambda e: e.reciprocal(c_e[:, :, :], c_e[:, :, :]), "dve")
    dve.wait(m)
    m = dve.do(lambda e: e.tensor_tensor(c_e[:, :, :], c_e[:, :, :], c_sb[:, :, :], op=ALU.mult), "dve")
    ident_ready = dve.do(lambda e: e.tensor_copy(ident_bf[:, :], ident), "dve")
    bank = take()
    pe.wait(m, loaded_first)
    for j in range(2):
        m = pe.do(lambda e, j=j, v=bank.view: e.transpose(v[:, j * B:(j + 1) * B], c_e[:, j, :], ident[0:B, 0:B]), "pe")
    act.wait(m)
    cT_ready = bank.free = act.do(lambda e, v=bank.view: e.copy(cT[:, :, :], v[:, 0:2 * B].rearrange("p (l b) -> p l b", b=B)), "act")

    bank = take()
    pe.wait(cT_ready)
    mod_view = bank.view[:, 0:2 * 4 * B].rearrange("p (l j b) -> p l j b", l=2, j=4)
    for l in range(2):
        for j, six in enumerate((0, 1, 3, 4)):
            m = pe.do(lambda e, l=l, j=j, six=six, v=mod_view: e.matmul(
                v[:, l, j, :], wmod[l][:, six, :], cT[:, l, :], start=True, stop=True), "pe")
    dve.wait(m)
    dve.do(lambda e, v=mod_view: e.tensor_copy(modT[:, :, 0::2, :], v[:, :, 0::2, :]), "dve")
    mod_ready = bank.free = dve.do(lambda e, v=mod_view: e.tensor_scalar(
        modT[:, :, 1::2, :], v[:, :, 1::2, :], 1.0, None, ALU.add), "dve")

    bank = take()
    gate_view = bank.view[0:B, :].rearrange("p (j c) -> p j c", c=C)
    for l in range(2):
        for j, six in enumerate((2, 5)):
            m = pe.do(lambda e, l=l, j=j, six=six, v=gate_view: e.matmul(
                v[:, 2 * l + j, :], cT[:, l, :], wmod[l][:, six, :], start=True, stop=True), "pe")
    dve.wait(m)
    dve.do(lambda e, v=gate_view: e.tensor_scalar(gate_s, v, 0.0, 2.0, ALU.is_ge, ALU.mult), "dve")
    m = bank.free = dve.do(lambda e, v=gate_view: e.tensor_copy(gate_sb[:, :, :], v), "dve")
    flat, sign2 = gate_sb[:, :, :].rearrange("p j c -> p (j c)"), gate_s.rearrange("p j c -> p (j c)")
    dve.wait(m)
    m = dve.do(lambda e: e.scalar_tensor_tensor(flat, sign2, -1.0, flat, ALU.add, ALU.mult), "dve")
    dve.wait(m)
    m = dve.do(lambda e: e.tensor_scalar(flat, flat, 0.25, None, ALU.max), "dve")
    dve.wait(m)
    gate_ready = dve.do(lambda e: e.scalar_tensor_tensor(flat, sign2, -1.0, flat, ALU.add, ALU.mult), "dve")

    bank = take()
    m = pe.do(lambda e, v=bank.view: e.transpose(v[0:D0, 0:C], wvd[:, :], ident), "pe")
    act.wait(m)
    m = bank.free = act.do(lambda e, v=bank.view: e.copy(wvdT[:, :], v[0:D0, 0:C]), "act")
    bank = take()
    pe.wait(m)
    m = pe.do(lambda e, v=bank.view: e.matmul(v[:, 0:C], wvdT[:, :], wvu[:, :], start=True, stop=True), "pe")
    act.wait(m)
    wv0_ready = bank.free = act.do(lambda e, v=bank.view: e.copy(wv0[:, :], v[:, 0:C]), "act")
    act.wait(loaded_rest)
    wqk0_ready = act.do(lambda e: e.mul(wqk0[:, 0:D0], wqk0[:, 0:D0], D0 ** -0.5), "act")

    pe.wait(loaded_rest)
    bank = take()
    for j in range(4):
        m = pe.do(lambda e, j=j, v=bank.view: e.transpose(v[:, j * P:(j + 1) * P], w_nat[:, j, :], ident), "pe")
    act.wait(m)
    act.do(lambda e, v=bank.view: e.mul(wT1[:, 0:2, :], v[:, 0:2 * P].rearrange("p (j h) -> p j h", h=P), DH ** -0.25), "act")
    wT1_ready = bank.free = act.do(lambda e, v=bank.view: e.copy(
        wT1[:, 2:4, :], v[:, 2 * P:].rearrange("p (j h) -> p j h", h=P)), "act")
    bank = take()
    m = pe.do(lambda e, v=bank.view: e.transpose(v[:, 0:B * KC], b1_nat[:, :], ident[0:B * KC, 0:B * KC]), "pe")
    act.wait(m)
    b1T_ready = bank.free = act.do(lambda e, v=bank.view: e.copy(b1T[:, :], v[:, 0:B * KC]), "act")

    dve.wait(loaded_rest)
    m = dve.do(lambda e: e.tensor_copy(be_parts[:, 0, :], be_f[:, :]), "dve")
    dve.wait(m)
    m = dve.do(lambda e: e.tensor_tensor(be_r[:, :], be_f[:, :], be_parts[:, 0, :], op=ALU.subtract), "dve")
    dve.wait(m)
    m = dve.do(lambda e: e.tensor_copy(be_parts[:, 1, :], be_r[:, :]), "dve")
    dve.wait(m)
    m = dve.do(lambda e: e.tensor_tensor(be_parts[:, 2, :], be_r[:, :], be_parts[:, 1, :], op=ALU.subtract), "dve")
    sp.wait(m)
    for j in range(PARTS):
        be3_ready = sp.dma(be3[j * EXPERTS:(j + 1) * EXPERTS, :], be_parts[:, j, :], "be3")

    def normalize(src, ready, xn, xn_free, st, mv, sm):
        dve.wait(*ready)
        for t in range(T):
            m = dve.do(lambda e, t=t: e.bn_stats(st[:, t, :], src[:, t, :]), "dve")
        dve.wait(m)
        for t in range(T):
            m = dve.do(lambda e, t=t: e.bn_aggr(mv[:, t, :], st[:, t, :]), "dve")
        yield
        pool.wait(m, mh_ready)
        pool.do(lambda e: e.tensor_scalar(sm[:, 0, :], mv[:, :, 0], -1.0, 0.0, ALU.mult, ALU.add), "pool")
        m = pool.do(lambda e: e.tensor_scalar(sm[:, 1, :], mv[:, :, 1], 1.0, EPS, ALU.mult, ALU.add), "pool")
        pool.wait(m)
        m = pool.do(lambda e: e.tensor_tensor(sm[:, 2, :], sm[:, 1, :], minus_half[:, :], op=ALU.pow), "pool")
        pool.wait(m, xn_free)
        for t in range(T):
            m = pool.do(lambda e, t=t: e.tensor_scalar(
                xn[:, t, :], src[:, t, :], sm[:, 0, t:t + 1], sm[:, 2, t:t + 1], ALU.add, ALU.mult), "pool")
        yield
        return m

    def to_channels(xn, xn_ready, hT, hT_free, block, which, b):
        pe.wait(xn_ready, mod_ready)
        for half in range(HALVES):
            bank = take()
            for j in range(4):
                m = pe.do(lambda e, t=4 * half + j, o=bank.view[:, j * P:(j + 1) * P]: e.transpose(
                    o, xn[:, t, :], ident), "pe" if j == 3 else None)
            act.wait(m, hT_free, mod_ready)
            r = bank.free = act.do(lambda e, half=half, v=bank.view: e.activation(
                hT[:, half * BANK:(half + 1) * BANK], v, ACT.Identity,
                scale=modT[:, block, which + 1, b:b + 1], bias=modT[:, block, which, b:b + 1]), "act")
            yield
        return r, m

    state = {"hT_f": None, "xn_f": None, "rest": None, "wv0b": None, "ops0": None, "v0": None, "s0": [None, None],
             "p0T": [None, None], "onehotT": None, "hm": [None, None], "parts1": [None, None],
             "hT_b": wv0_ready, "xn_b": None, "w12": None, "qk0": None,
             "parts_read": [None, None]}
    gates_ready, qkv_ready, v1_ready, x2_ready = {}, {}, {}, {}
    gates_done, v1_done, nd_done = {-3: None, -2: None, -1: None}, {-2: None, -1: None}, {-1: gate_ready}

    def split_rest(parts, r, r_ready, rows):
        pool.wait(*r_ready)
        m = pool.do(lambda e: e.tensor_scalar(parts[0:rows, 1, :], r[0:rows, :], 1.0, 0.0, ALU.mult, ALU.add), "pool")
        pool.wait(m)
        return pool.do(lambda e: e.tensor_tensor(parts[0:rows, 2, :], r[0:rows, :], parts[0:rows, 1, :], op=ALU.subtract), "pool")

    def front(b):
        x, gate = xs[b % 4], gates[b % 3]
        bank = take()
        pe.wait(gate_ready, loaded_rest)
        m = pe.do(lambda e, v=bank.view: e.matmul(v, sel[:, b, :], gate_sb[:, :, :].rearrange("p j c -> p (j c)"),
                                                  start=True, stop=True), "pe")
        act.wait(m, gates_done[b - 3])
        gates_ready[b] = bank.free = act.do(lambda e, v=bank.view: e.copy(gate[:, :, :].rearrange("p j c -> p (j c)"), v), "act")
        pool.wait(gates_ready[b], wv0_ready, state["wv0b"])
        wv0b_ready = pool.do(lambda e: e.tensor_tensor(wv0b[:, :], wv0[:, :], gate[:, 0, :], op=ALU.mult), "pool")
        yield

        xn_ready = yield from normalize(x, [x_loaded[b]], xn_f, state["xn_f"], st_f, mv_f, sm_f)
        hT_ready, state["xn_f"] = yield from to_channels(xn_f, xn_ready, hT_f, state["hT_f"], 0, 0, b)
        for half in range(HALVES):
            cols = slice(half * BANK, (half + 1) * BANK)
            bank = take()
            pe.wait(hT_ready, wqk0_ready)
            m = pe.do(lambda e, cols=cols, v=bank.view: e.matmul(v[0:2 * D0, :], wqk0[:, :], hT_f[:, cols], start=True, stop=True), "pe")
            act.wait(m, state["qk0"], state["parts1"][0])
            m = act.do(lambda e, cols=cols, v=bank.view: e.copy(qk0_parts[:, 0, cols], v[0:2 * D0, :]), "act")
            dve.wait(m, state["rest"])
            m = bank.free = dve.do(lambda e, cols=cols, v=bank.view: e.tensor_tensor(
                rest[0:2 * D0, cols], v[0:2 * D0, :], qk0_parts[:, 0, cols], op=ALU.subtract), "dve")
            yield
        m = state["rest"] = split_rest(qk0_parts, rest, [m], 2 * D0)
        sp.wait(m, state["ops0"], state["parts1"][1])
        lo, hi = qk0_parts[0:D0, :, :], qk0_parts[D0:2 * D0, :, :]
        for dst, src in ((q0_ops[0:D0, :, :], lo[:, 0:2, :]), (q0_ops[D0:2 * D0, 0, :], lo[:, 1, :]),
                         (q0_ops[D0:2 * D0, 1, :], lo[:, 0, :]), (q0_ops[2 * D0:, :, :], lo[:, 0:3:2, :]),
                         (k0_ops[0:D0, :, :], hi[:, 0:2, :]), (k0_ops[D0:2 * D0, :, :], hi[:, 0:2, :]),
                         (k0_ops[2 * D0:, 0, :], hi[:, 2, :]), (k0_ops[2 * D0:, 1, :], hi[:, 0, :])):
            ops0_ready = state["qk0"] = sp.dma(dst, src, "first_block_ops")
        yield
        for half in range(HALVES):
            bank = take()
            pe.wait(hT_ready, wv0b_ready)
            for j in range(4):
                t = 4 * half + j
                m = pe.do(lambda e, t=t, o=bank.view[:, j * C:(j + 1) * C]: e.matmul(
                    o, hT_f[:, t * P:(t + 1) * P], wv0b[:, :], start=True, stop=True), "pe" if j == 3 else None)
            act.wait(m, state["v0"])
            v0_ready = bank.free = act.do(lambda e, half=half, v=bank.view: e.copy(
                v0[:, 4 * half:4 * half + 4, 0:C], v.rearrange("p (t c) -> p t c", c=C)), "act")
            yield
        state["wv0b"] = state["hT_f"] = m
        pool.wait(v0_ready, v0_ones, state["v0"])
        m = pool.do(lambda e: e.tensor_scalar(v0_later[:, T - 2, :], v0[:, T - 1, :], 1.0, 0.0, ALU.mult, ALU.add), "pool")
        for i in range(T - 3, -1, -1):
            pool.wait(m)
            m = pool.do(lambda e, i=i: e.tensor_tensor(v0_later[:, i, :], v0_later[:, i + 1, :], v0[:, i + 1, :], op=ALU.add), "pool")
        later_ready = m
        yield

        s_ready, p_ready, pT_ready = {}, {}, {}

        def scores(i):
            s, n = s0[i % 2], (i + 1) * P
            pool.wait(state["s0"][i % 2])
            if i < T - 1:
                marks = [pool.do(lambda e: e.memset(s[:, 0:P], NEG), "pool")]
            else:
                marks = []
            for c in range(0, n, BANK):
                w = min(BANK, n - c)
                bank = take()
                pe.wait(ops0_ready)
                for half in range(2):
                    m = pe.do(lambda e, half=half, c=c, w=w, v=bank.view: e.matmul(
                        v[:, 0:w], q0_ops[:, half, i * P:(i + 1) * P], k0_ops[:, half, c:c + w],
                        start=half == 0, stop=half == 1), "pe" if half else None)
                state["ops0"] = m
                act.wait(m, state["s0"][i % 2])
                m = bank.free = act.do(lambda e, c=c, w=w, v=bank.view: e.copy(s[:, P + c:P + c + w], v[:, 0:w]), "act")
                yield
            pool.wait(m)
            marks.append(pool.do(lambda e: e.tensor_tensor(s[:, n:n + P], s[:, n:n + P], tril, op=ALU.mult), "pool"))
            s_ready[i] = marks

        def softmax(i):
            s, n = s0[i % 2], (i + 1) * P
            dve.wait(*s_ready[i], state["rest"])
            m = dve.do(lambda e: e.tensor_scalar(rest[:, 0:n], s[:, P:P + n], 0.0, NEG, ALU.is_equal, ALU.mult), "dve")
            dve.wait(m)
            m = dve.do(lambda e: e.tensor_tensor_reduce(
                out=s[:, P:P + n], in0=s[:, P:P + n], in1=rest[:, 0:n], scale=1.0, scalar=NEG,
                op0=ALU.add, op1=ALU.max, accum_out=mx0[:, i:i + 1]), "dve")
            state["rest"] = m
            dve.wait(m)
            m = dve.do(lambda e: e.tensor_scalar(nm0[:, i:i + 1], mx0[:, i:i + 1], -1.0, None, ALU.mult), "dve")
            first = P if i == T - 1 else 0
            act.wait(m, *s_ready[i])
            p_ready[i] = act.do(lambda e: e.activation(s[:, first:P + n], s[:, first:P + n], ACT.Exp, bias=nm0[:, i:i + 1]), "act")

        def transpose_p(i):
            s, pT = s0[i % 2], p0T[0]
            blocks = list(range(1 if i == T - 1 else 0, i + 2))
            for c in range(0, len(blocks), 4):
                some = blocks[c:c + 4]
                bank = take()
                pe.wait(p_ready[i])
                for j, k in enumerate(some):
                    m = pe.do(lambda e, k=k, o=bank.view[:, j * P:(j + 1) * P]: e.transpose(
                        o, s[:, k * P:(k + 1) * P], ident), "pe" if k == some[-1] else None)
                on = act if (i + c // 4) % 2 else dve
                on.wait(m, state["p0T"][0])
                dst, src = pT[:, some[0]:some[-1] + 1, :].rearrange("p k q -> p (k q)"), bank.view[:, 0:len(some) * P]
                r = bank.free = on.do((lambda e, dst=dst, src=src: e.copy(dst, src)) if on is act else
                                      (lambda e, dst=dst, src=src: e.tensor_copy(dst, src)), "act" if on is act else "dve")
                pT_ready.setdefault(i, []).append(r)
                yield
            state["s0"][i % 2] = m

        def times_v(i):
            pT = p0T[0]
            bank = take()
            pe.wait(*pT_ready[i], v0_ready, v0_ones, later_ready)
            o = bank.view[:, 0:C + 1]
            for k in range(i + 1):
                m = pe.do(lambda e, k=k: e.matmul(o, pT[:, k + 1, :], v0[:, k, :], start=k == 0, stop=i == T - 1 and k == i),
                          "pe" if i == T - 1 and k == i else None)
            if i < T - 1:
                m = pe.do(lambda e: e.matmul(o, pT[:, 0, :], v0_later[:, i, :], start=False, stop=True), "pe")
            state["p0T"][0] = state["v0"] = m
            dve.wait(m)
            m = dve.do(lambda e: e.reciprocal(rs0[:, i:i + 1], o[:, C:C + 1]), "dve")
            dve.wait(m)
            bank.free = dve.do(lambda e: e.scalar_tensor_tensor(
                x[:, i, :], o[:, 0:C], rs0[:, i:i + 1], x[:, i, :], ALU.mult, ALU.add), "dve")
            yield
            return bank.free

        for n in range(T + 3):
            if n >= 3:
                x1_ready = yield from times_v(n - 3)
            if 2 <= n < T + 2:
                yield from transpose_p(n - 2)
            if 1 <= n < T + 1:
                softmax(n - 1)
            if n < T:
                yield from scores(n)

        xn_ready = yield from normalize(x, [x1_ready], xn_f, state["xn_f"], st_f, mv_f, sm_f)
        hT_ready, state["xn_f"] = yield from to_channels(xn_f, xn_ready, hT_f, state["hT_f"], 0, 2, b)
        logits = xn_f
        for half in range(HALVES):
            bank = take()
            pe.wait(hT_ready, loaded_rest)
            for j in range(4):
                t = 4 * half + j
                m = pe.do(lambda e, t=t, o=bank.view[:, j * C:(j + 1) * C]: e.matmul(
                    o, hT_f[:, t * P:(t + 1) * P], wg[:, :], start=True, stop=True), "pe" if j == 3 else None)
            dve.wait(m, state["xn_f"], loaded_rest)
            lg = bank.free = dve.do(lambda e, half=half, v=bank.view: e.tensor_tensor(
                logits[:, 4 * half:4 * half + 4, :], v.rearrange("p (t c) -> p t c", c=C),
                bg_rows[:, :].unsqueeze(1).broadcast_to([P, 4, C]), op=ALU.add), "dve")
            yield
        dve.wait(lg)
        for t in range(T):
            m = dve.do(lambda e, t=t: e.max(top8[:, t, :], logits[:, t, :]), "dve")
        pool.wait(m)
        ng = pool.do(lambda e: e.tensor_scalar(ngmx[:, :], top8[:, :, 0], -1.0, 0.0, ALU.mult, ALU.add), "pool")
        yield
        dve.wait(m)
        for t in range(T):
            m = dve.do(lambda e, t=t: e.max_index(idx8[:, t, :], top8[:, t, :], logits[:, t, :]), "dve")
        dve.wait(m)
        em = dve.do(lambda e: e.tensor_scalar(eidx[:, :], idx8[:, :, 0], EXPERTS - 1, None, ALU.bitwise_and), "dve")
        dve.wait(em)
        em = dve.do(lambda e: e.tensor_copy(eidx_f[:, :], eidx[:, :]), "dve")
        dve.wait(em, state["onehotT"])
        oh_ready = dve.do(lambda e: e.tensor_tensor(
            onehot[:, :, :, :].rearrange("p t r e -> p t (r e)").rearrange("p t (r e) -> p t r e", r=PARTS),
            iota8.unsqueeze(1).unsqueeze(1).broadcast_to([P, T, PARTS, EXPERTS]),
            eidx_f[:, :].unsqueeze(2).unsqueeze(3).broadcast_to([P, T, PARTS, EXPERTS]), op=ALU.is_equal), "dve")
        act.wait(m, ng, lg)
        for t in range(T):
            m = act.do(lambda e, t=t: e.activation(logits[:, t, :], logits[:, t, :], ACT.Exp,
                                                   bias=ngmx[:, t:t + 1], accum_out=gsum[:, t:t + 1]), "act")
        dve.wait(m)
        exp_done = m
        gp_ready = dve.do(lambda e: e.reciprocal(gp[:, :], gsum[:, :]), "dve")
        yield
        bank = take()
        pe.wait(oh_ready, ident_ready)
        ohT = bank.view.bitcast(BF16)
        for t in range(T):
            m = pe.do(lambda e, t=t: e.transpose(ohT[0:PARTS * EXPERTS, t * P:(t + 1) * P],
                                                 onehot[:, t, :, :].rearrange("p r e -> p (r e)"), ident_bf[:, :]),
                      "pe" if t == T - 1 else None)
        act.wait(m, state["onehotT"])
        ohT_ready = bank.free = act.do(lambda e: e.copy(onehotT[:, :], ohT[0:PARTS * EXPERTS, :]), "act")
        yield
        picked = xn_f
        for t in range(T):
            for quad in range(EXPERTS // 4):
                bank = take()
                for j in range(4):
                    m = pe.do(lambda e, k=4 * quad + j, o=bank.view[:, j * P:(j + 1) * P]: e.matmul(
                        o, onehot[:, t, 0, k:k + 1].broadcast_to([P, P]), ident_bf[:, :], start=True, stop=True),
                        "pe" if j == 3 else None)
                dve.wait(m, state["hm"][quad])
                hm_ready = bank.free = dve.do(lambda e, quad=quad, t=t, v=bank.view: e.tensor_tensor(
                    hm[:, 4 * quad:4 * quad + 4, :], v.rearrange("p (k q) -> p k q", q=P),
                    hT_f[:, t * P:(t + 1) * P].unsqueeze(1).broadcast_to([C, 4, P]), op=ALU.mult), "dve")
                if quad:
                    yield
            bank = take()
            o = bank.view[:, 0:C]
            pe.wait(ohT_ready, be3_ready)
            pe.do(lambda e, t=t: e.matmul(o, onehotT[:, t * P:(t + 1) * P], be3[:, :], start=True, stop=False))
            pe.wait(hm_ready)
            for k in range(EXPERTS):
                m = pe.do(lambda e, k=k: e.matmul(o, hm[:, k, :], we[:, k, :], start=False, stop=k == EXPERTS - 1),
                          "pe" if k % 4 == 3 else None)
                if k % 4 == 3:
                    state["hm"][k // 4] = m
            act.wait(m, gp_ready, exp_done)
            r = bank.free = act.do(lambda e, t=t: e.activation(picked[:, t, :], o, ACT.Relu, scale=gp[:, t:t + 1]), "act")
            yield
            if t % 4 == 3:
                tiles = slice(t - 3, t + 1)
                pool.wait(r)
                g = pool.do(lambda e, tiles=tiles: e.tensor_tensor(
                    picked[:, tiles, :], picked[:, tiles, :], gate[:, 1, :].unsqueeze(1).broadcast_to([P, 4, C]), op=ALU.mult), "pool")
                pool.wait(g)
                x2 = pool.do(lambda e, tiles=tiles: e.tensor_tensor(x[:, tiles, :], x[:, tiles, :], picked[:, tiles, :], op=ALU.add), "pool")
        state["hT_f"] = state["onehotT"] = m
        state["xn_f"] = x2
        yield

        xn_ready = yield from normalize(x, [x2], xn_f, state["xn_f"], st_f, mv_f, sm_f)
        x2_ready[b] = xn_ready
        hT_ready, state["xn_f"] = yield from to_channels(xn_f, xn_ready, hT_f, state["hT_f"], 1, 0, b)
        rests = (rest, xn_f[:, :, :].rearrange("p t c -> p (t c)"))
        for w, parts in enumerate(qk1_parts):
            r = rests[w]
            for half in range(HALVES):
                cols = slice(half * BANK, (half + 1) * BANK)
                bank = take()
                pe.wait(hT_ready, wT1_ready)
                m = pe.do(lambda e, w=w, cols=cols, v=bank.view: e.matmul(v, wT1[:, w, :], hT_f[:, cols], start=True, stop=True), "pe")
                act.wait(m, state["parts1"][w], state["ops0"] if w else state["qk0"])
                m = act.do(lambda e, cols=cols, v=bank.view, parts=parts: e.copy(parts[:, 0, cols], v), "act")
                dve.wait(m, state["rest"] if w == 0 else state["xn_f"])
                m = bank.free = dve.do(lambda e, cols=cols, v=bank.view, parts=parts, r=r: e.tensor_tensor(
                    r[:, cols], v, parts[:, 0, cols], op=ALU.subtract), "dve")
                yield
            m = split_rest(parts, r, [m], P)
            if w == 0:
                state["rest"] = m
            else:
                state["xn_f"] = m
            sp.wait(m, state["parts_read"][b % 2])
            state["parts1"][w] = sp.dma(parts_dram[b % 2, w].rearrange("r p n -> p r n"), parts[:, :, :], f"parts{w}")
        qkv_ready[b] = list(state["parts1"])
        for half in range(HALVES):
            bank = take()
            for j in range(4):
                t = 4 * half + j
                m = pe.do(lambda e, t=t, o=bank.view[:, j * P:(j + 1) * P]: e.matmul(
                    o, hT_f[:, t * P:(t + 1) * P], wT1[:, 2, :], start=True, stop=True), "pe" if j == 3 else None)
            act.wait(m, v1_done[b - 2])
            v1_ready[b] = bank.free = act.do(lambda e, half=half, v=bank.view: e.copy(
                v1[b % 2][:, 4 * half:4 * half + 4, :, 0:DH], v.rearrange("p (t h d) -> p t h d", t=4, d=DH)), "act")
            yield
        state["hT_f"] = m

    slot_free, ops_ready, m_ready = [None] * SLOTS, {}, {}

    def load_operands(g):
        b, slot, h0 = g // GROUPS, g % SLOTS, (g % GROUPS) * GROUP
        sp.wait(*qkv_ready[b], slot_free[slot], q_zero, k_ready)
        for w, (ops, which) in enumerate(((q_ops, Q_PART), (k_ops, K_PART))):
            for r, part in enumerate(which):
                src = parts_dram[b % 2, w, part, h0 * DH:(h0 + GROUP) * DH, :].rearrange("(h d) n -> d h n", d=DH)
                ops_ready[g] = sp.dma(ops[r * DH:(r + 1) * DH, slot, :, :], src, f"operands{slot}")
        state["parts_read"][b % 2] = ops_ready[g]

    mx_free = [None, None]
    mx_ready = {}

    def maxima(pair):
        g = pair // 2
        slot = g % SLOTS
        for hh in range(2):
            h = 2 * (pair % 2) + hh
            for i in range(T):
                for half in range(HALVES):
                    bank = shared.take()
                    pe.wait(bank.free, ops_ready[g])
                    m = pe.do(lambda e, h=h, i=i, half=half, v=bank.view: e.matmul(
                        v, q_ops[0:K_MAX, slot, h, i * P:(i + 1) * P], k_ops[0:K_MAX, slot, h, half * BANK:(half + 1) * BANK],
                        start=True, stop=True), "pe_max")
                    dve.wait(m, mx_free[g % 2])
                    bank.free = mx_ready[g] = dve.do(lambda e, h=h, i=i, half=half, v=bank.view: e.tensor_reduce(
                        mx[g % 2][:, h * T + i, half:half + 1], v, axis=AX.X, op=ALU.max), "dve")
                    yield

    nm_parts_free = [None, None]
    nm_free = [None, None]

    def subtract_maxima(g):
        parts, slot = nm_parts[g % 2], g % SLOTS
        dve.wait(mx_ready[g], nm_free[0])
        mx_free[g % 2] = m = dve.do(lambda e: e.tensor_reduce(nm[:, :], mx[g % 2][:, :, :], axis=AX.X, op=ALU.max, negate=True), "dve")
        yield
        bank = shared.take()
        pe.wait(bank.free, m)
        nm_free[0] = m = pe.do(lambda e: e.transpose(bank.view[0:GROUP * T, 0:P], nm[:, :], ident), "pe")
        act.wait(m, nm_parts_free[g % 2], nm_free[1])
        hi = act.do(lambda e: e.copy(parts[:, 0, :], bank.view[0:GROUP * T, 0:P]), "act")
        bank.free = m = act.do(lambda e: e.copy(nm_f[:, :], bank.view[0:GROUP * T, 0:P]), "act")
        yield
        pool.wait(m, hi)
        m = pool.do(lambda e: e.tensor_tensor(nm_r[:, :], nm_f[:, :], parts[:, 0, :], op=ALU.subtract), "pool")
        pool.wait(m)
        m = pool.do(lambda e: e.tensor_scalar(parts[:, 1, :], nm_r[:, :], 1.0, 0.0, ALU.mult, ALU.add), "pool")
        pool.wait(m)
        nm_free[1] = m = pool.do(lambda e: e.tensor_tensor(parts[:, 2, :], nm_r[:, :], parts[:, 1, :], op=ALU.subtract), "pool")
        sp.wait(m)
        for j in range(PARTS):
            dst = q_ops[K_MAX + j:K_MAX + j + 1, slot, :, :].rearrange("o h (i q) -> o (h i) q", q=P)
            m_ready[g] = nm_parts_free[g % 2] = sp.dma(dst, parts[:, j, :], f"maxima{g % 2}")
        yield

    p_free = [None] * 4
    o_free = [be3_ready]
    nd_ready = {}
    exps = {}

    def score_step(step, hh):
        pair, kb = divmod(step, T)
        g = pair // 2
        slot, h = g % SLOTS, 2 * (pair % 2) + hh
        banks = score_banks[hh]
        pe.wait(banks[0].free, banks[1].free, m_ready[g])
        for half in range(HALVES):
            m = pe.do(lambda e, half=half: e.matmul(
                banks[half].view, k_ops[0:K_EXP, slot, h, kb * P:(kb + 1) * P],
                q_ops[0:K_EXP, slot, h, half * BANK:(half + 1) * BANK], start=True, stop=True), "pe_scores" if half else None)
        if kb == T - 1 and pair % 2 and hh:
            slot_free[slot] = m
        buf = (2 * step + hh) % 4
        act.wait(m, p_free[buf])
        banks[0].free = banks[1].free = exps[step, hh] = act.do(
            lambda e: e.activation(p_sb[buf][:, :], score_psum[hh][:, :], ACT.Exp), "act_exp")

    def value_step(step):
        pair, kb = divmod(step, T)
        b, hp = divmod(pair, HEADS // 2)
        v = v1[b % 2]
        if kb == 0:
            pe.wait(pv_bank.free, v1_ready[b], v1_ones)
        pe.wait(exps[step, 0], exps[step, 1])
        for hh in range(2):
            buf = (2 * step + hh) % 4
            for half in range(HALVES):
                q = 32 * (2 * hh + half)
                m = pe.do(lambda e, hh=hh, half=half, q=q, buf=buf: e.matmul(
                    pv_psum[q:q + VW, :], v[:, kb, 2 * hp + hh, :], p_sb[buf][:, half * BANK:(half + 1) * BANK],
                    start=kb == 0, stop=kb == T - 1), "pe_pv" if half else None)
            p_free[buf] = m
        if kb < T - 1:
            return
        if hp == HEADS // 2 - 1:
            v1_done[b] = m
        dve.wait(m, o_free[0])
        pv_bank.free = m = dve.do(lambda e: e.tensor_copy(o_sb[:, :], pv_psum[:, :]), "dve")
        sp.wait(m, nd_done[b - 1])
        for hh in range(2):
            for half in range(HALVES):
                q, r = 32 * (2 * hh + half), (2 * hp + hh) * DH
                for j in range(2):
                    o_free[0] = nd_ready[b] = sp.dma(nd[r:r + DH, j, half * BANK:(half + 1) * BANK],
                                                     o_sb[q + j * DH:q + (j + 1) * DH, :], "attention_out")

    stored = {}

    def back_weights(b):
        gate = gates[b % 3]
        sp.wait(state["w12"], wT1_ready, gate_ready)
        sp.dma(w1_sb[:, :, :], W1[b].rearrange("(k o) c -> o k c", o=P), "in_w12")
        w12 = sp.dma(w2_sb[:, :], W2[b], "in_w12")
        pool.wait(gates_ready[b], wT1_ready, state["woutb"])
        pool.do(lambda e: e.tensor_tensor(woutb[:, :], wT1[:, 3, :], gate[:, 2, :], op=ALU.mult), "pool")
        wb = pool.do(lambda e: e.tensor_tensor(boutb[:, :], bout_rows[:, :], gate[:, 2, :], op=ALU.mult), "pool")
        yield
        bank = take()
        pe.wait(w12)
        for j in range(KC):
            m = pe.do(lambda e, j=j, o=bank.view[:, j * P:(j + 1) * P]: e.transpose(o, w2_sb[:, j * P:(j + 1) * P], ident),
                      "pe" if j == KC - 1 else None)
        act.wait(m, state["w12"])
        m = bank.free = act.do(lambda e, v=bank.view: e.copy(w2T[:, :, :].rearrange("p k c -> p (k c)"), v), "act")
        yield
        bank = take()
        pe.wait(m, b1T_ready)
        v = bank.view[:, 0:2 * C]
        for j in range(KC):
            pe.do(lambda e, j=j: e.matmul(v[:, 0:C], w1_sb[:, j, :], w2T[:, j, :], start=j == 0, stop=j == KC - 1))
        for j in range(KC):
            col = b1T[:, b * KC + j:b * KC + j + 1].broadcast_to([P, P])
            pe.do(lambda e, j=j, col=col: e.matmul(v[:, C:2 * C], col, w2T[:, j, :], start=j == 0, stop=False))
        state["w12"] = m = pe.do(lambda e: e.matmul(v[:, C:2 * C], sel[:, b, :], b2_sb[:, :], start=False, stop=True), "pe")
        dve.wait(m, gates_ready[b], state["wff"])
        wff_ready = bank.free = dve.do(lambda e: e.tensor_tensor(
            wff[:, :, :], v.rearrange("p (j c) -> p j c", c=C), gate[:, 3, :].unsqueeze(1).broadcast_to([P, 2, C]), op=ALU.mult), "dve")
        gates_done[b] = wff_ready
        yield
        return wb, wff_ready

    def rows(tile):
        return tile.unsqueeze(1).broadcast_to([P, T, C])

    def back(b):
        x = xs[b % 4]
        wb, wff_ready = yield from back_weights(b)
        dve.wait(nd_ready[b])
        m = dve.do(lambda e: e.reciprocal(nd[:, 1, :], nd[:, 1, :]), "dve")
        pool.wait(m, nd_ready[b])
        aT_ready = pool.do(lambda e: e.tensor_tensor(nd[:, 0, :], nd[:, 0, :], nd[:, 1, :], op=ALU.mult), "pool")
        pool.wait(wb, x2_ready[b])
        xb = pool.do(lambda e: e.tensor_tensor(x[:, :, :], x[:, :, :], rows(boutb[:, :]), op=ALU.add), "pool")
        yield
        for half in range(HALVES):
            bank = take()
            pe.wait(aT_ready, wb)
            for j in range(4):
                t = 4 * half + j
                m = pe.do(lambda e, t=t, o=bank.view[:, j * C:(j + 1) * C]: e.matmul(
                    o, nd[:, 0, t * P:(t + 1) * P], woutb[:, :], start=True, stop=True), "pe" if j == 3 else None)
            dve.wait(m, xb)
            x3 = bank.free = dve.do(lambda e, half=half, v=bank.view: e.tensor_tensor(
                x[:, 4 * half:4 * half + 4, :], v.rearrange("p (t c) -> p t c", c=C), x[:, 4 * half:4 * half + 4, :], op=ALU.add), "dve")
            yield
        nd_done[b] = state["woutb"] = m
        xn_ready = yield from normalize(x, [x3], xn_b, state["xn_b"], st_b, mv_b, sm_b)
        pool.wait(wff_ready, xn_ready)
        xb = pool.do(lambda e: e.tensor_tensor(x[:, :, :], x[:, :, :], rows(wff[:, 1, :]), op=ALU.add), "pool")
        hT_ready, state["xn_b"] = yield from to_channels(xn_b, xn_ready, hT_b, state["hT_b"], 1, 2, b)
        for half in range(HALVES):
            bank = take()
            pe.wait(hT_ready, wff_ready)
            for j in range(4):
                t = 4 * half + j
                m = pe.do(lambda e, t=t, o=bank.view[:, j * C:(j + 1) * C]: e.matmul(
                    o, hT_b[:, t * P:(t + 1) * P], wff[:, 0, :], start=True, stop=True), "pe" if j == 3 else None)
            dve.wait(m, xb)
            y = bank.free = dve.do(lambda e, half=half, v=bank.view: e.tensor_tensor(
                x[:, 4 * half:4 * half + 4, :], v.rearrange("p (t c) -> p t c", c=C), x[:, 4 * half:4 * half + 4, :], op=ALU.add), "dve")
            yield
        state["hT_b"] = state["wff"] = m
        sp.wait(y)
        stored[b] = sp.dma(out[b].rearrange("(t p) c -> p t c", p=P), x[:, :, :], f"out{b % 2}")
    state["woutb"] = state["wff"] = None

    for _ in front(0):
        pass
    load_x(2)
    ring[0] = shared

    done, now = {"front": 0}, [0]
    FRONT_FROM = -T * HEADS // 4

    def fronts():
        for b in range(1, B):
            while now[0] < FRONT_FROM + (b - 1) * T * HEADS // 2:
                yield
            yield from front(b)
            done["front"] = b

    def backs(b):
        yield from back(b)
        if b + 4 < B:
            load_x(b + 4, stored[b])

    beside = []
    PAIRS = B * HEADS // 2
    front_pieces = 96

    def advance(share):
        for job in list(beside):
            job[2] += job[1] * share
            while job[2] >= 1:
                job[2] -= 1
                if next(job[0], "end") == "end":
                    beside.remove(job)
                    break

    fronts_job = [fronts(), front_pieces / 64, 0.0]
    beside.append(fronts_job)
    load_x(3)
    max_steps = None
    for step in range(-LEAD * T, PAIRS * T + 1):
        pair, kb = divmod(step, T)
        now[0] = step
        lead = pair + LEAD
        if kb == 0 and lead < PAIRS:
            for g in ((0, 1) if lead == 0 else (lead // 2 + 1,) if lead % 2 else ()):
                if g < B * GROUPS and g not in ops_ready:
                    while done["front"] < g // GROUPS:
                        next(fronts_job[0])
                    load_operands(g)
            max_steps = maxima(lead)
        if step < 0 or step > PAIRS * T - 1:
            mains = [lambda: None] * 4
        else:
            mains = [lambda: score_step(step, 0), lambda: score_step(step, 1), lambda: None, lambda: None]
        if step > 0:
            mains[2] = lambda: value_step(step - 1)
        for n in range(4):
            if lead < PAIRS:
                next(max_steps, None)
            mains[n]()
            advance(0.25)
        if lead < PAIRS and kb == T - 1 and lead % 2:
            next(max_steps, None)
            beside.append([subtract_maxima(lead // 2), 1.0, 0.0])
        if step > 0 and step % (T * HEADS // 2) == 0:
            b = step // (T * HEADS // 2) - 1
            if b == B - 1:
                ring[0] = wide
            beside.append([backs(b), 1.0, 0.0])
    for job in list(beside):
        for _ in job[0]:
            pass

    sp.wait(*stored.values(), *state["parts1"])


NAMES = ["L0_attn_inputs", "L0_attn_Wq", "L0_attn_Wk", "L0_attn_Wvdown", "L0_attn_Wvup", "L0_ffn_Wg", "L0_ffn_bg",
         "L0_ffn_We", "L0_ffn_be", "L0_c", "L0_wmod", "L1_attn_Wq", "L1_attn_Wk", "L1_attn_Wv", "L1_attn_Wout",
         "L1_attn_bout", "L1_ffn_W1", "L1_ffn_b1", "L1_ffn_W2", "L1_ffn_b2", "L1_c", "L1_wmod"]


def kernel(**inputs):
    from contextlib import ExitStack
    import concourse.bacc as bacc
    from concourse.bass_utils import run_bass_kernel_spmd

    nc = bacc.Bacc("TRN2", target_bir_lowering=False, num_devices=1)
    arrays = {name: np.ascontiguousarray(inputs[name]) for name in NAMES}
    iota = np.broadcast_to(np.arange(EXPERTS, dtype=np.float32), (P, EXPERTS))
    arrays["consts"] = np.concatenate([np.eye(P, dtype=np.float32), np.tril(np.ones((P, P), np.float32)), iota], axis=1)
    arrays["select"] = np.repeat(np.eye(B, dtype=np.float32), P, axis=1)
    args = [nc.dram_tensor(f"in_{n}", a.shape, mybir.dt.from_np(a.dtype), kind="ExternalInput").ap() for n, a in arrays.items()]
    out = nc.dram_tensor("out", (B, N, C), F32, kind="ExternalOutput").ap()
    with ExitStack() as ctx:
        build(nc, ctx, *args, out)
    result = run_bass_kernel_spmd(nc, [{f"in_{n}": a for n, a in arrays.items()}], core_ids=[0])
    return result.results[0]["out"]
```

```python
import numpy as np
import concourse.bass as bass
import concourse.mybir as mybir

F32 = mybir.dt.float32
BF16 = mybir.dt.bfloat16
U32 = mybir.dt.uint32
ALU = mybir.AluOpType
ACT = mybir.ActivationFunctionType
AX = mybir.AxisListType

P = 128
B, N, C = 8, 1024, 128
T = N // P
D0 = 32
EXPERTS = 8
HEADS, DH = 16, 8
INTER = 512
KC = INTER // P
BANK = 512
HALVES = N // BANK
EPS = 1e-5
NEG = float(np.finfo(np.float32).min)
PARTS = 3
Q_PART = (0, 0, 0, 1, 1, 2)
K_PART = (0, 1, 2, 0, 1, 0)
K_MAX = 96
K_EXP = K_MAX + PARTS
GROUP = 4
GROUPS = HEADS // GROUP
SLOTS = 3
VW = DH + 1
LEAD = 14
FRONT_COST = 58.5
LEAD_IN_RATE = 1.5
SHARES = (0.35, 0.3, 0.1, 0.25)
BACK_RATE = 0.5
BACK_WEIGHTS_STEP = 44
EMPTY_AFTER = {"normalize": 6, "first block's operands": 5, "sums": 1, "numerators": 2}


BF16_ONES = float(np.array([0x3F803F80], np.uint32).view(np.float32)[0])


class Semaphores:

    def __init__(self, nc, ctx):
        self.nc, self.ctx, self.made, self.value = nc, ctx, {}, {}

    def mark(self, name, by):
        if name not in self.made:
            self.made[name] = self.ctx.enter_context(self.nc.semaphore(name))
            self.value[name] = 0
        self.value[name] += by
        return name, self.value[name]


class Queue:

    def __init__(self, engine, sems):
        self.engine, self.sems, self.reached = engine, sems, {}

    def wait(self, *marks):
        for m in marks:
            if m is not None and self.reached.get(m[0], 0) < m[1]:
                self.reached[m[0]] = m[1]
                self.engine.wait_ge(self.sems.made[m[0]], m[1])

    def raises(self, instruction, signal, by):
        if signal is None:
            return None
        m = self.sems.mark(signal, by)
        instruction.then_inc(self.sems.made[signal], by)
        return m

    def do(self, issue, signal=None):
        return self.raises(issue(self.engine), signal, 1)

    def dma(self, out, in_, signal):
        return self.raises(self.engine.dma_start(out, in_), signal, 16)


class Bank:

    def __init__(self, view):
        self.view, self.free = view, None


class Ring:
    def __init__(self, banks):
        self.banks, self.at = banks, 0

    def take(self):
        self.at += 1
        return self.banks[(self.at - 1) % len(self.banks)]


def finish(pieces):
    while True:
        try:
            next(pieces)
        except StopIteration as end:
            return end.value


def build(nc, ctx, x_in, Wq0, Wk0, Wvdown, Wvup, Wg, bg, We, be, c0, wmod0,
          Wq1, Wk1, Wv1, Wout, bout, W1, b1, W2, b2, c1, wmod1, consts, select, out):
    sems = Semaphores(nc, ctx)
    pe, act, dve, pool, sp = (Queue(e, sems) for e in (nc.tensor, nc.scalar, nc.vector, nc.gpsimd, nc.sync))

    engines = {"dve": dve, "pool": pool}

    def sb(name, shape, dt=F32):
        return ctx.enter_context(nc.sbuf_tensor(name, shape, dt))

    psum = [ctx.enter_context(nc.psum_tensor(f"psum{i}", [P, BANK], F32)) for i in range(8)]
    pv_psum = psum[0]
    pv_bank = Bank(pv_psum[:, :])
    ring = Ring([Bank(t[:, :]) for t in psum[1:]])

    def take():
        bank = ring.take()
        pe.wait(bank.free)
        return bank

    const_sb = sb("consts", [P, 2 * P + EXPERTS])
    ident, tril, iota8 = const_sb[:, 0:P], const_sb[:, P:2 * P], const_sb[:, 2 * P:]
    ident_bf = sb("ident_bf", [P, P], BF16)
    sel = sb("select", [B, B, P])
    minus_half = sb("minus_half", [P, T])

    wqk0 = sb("wqk0", [C, 2 * D0])
    wv0 = sb("wv0", [C, C])
    wg, we = sb("wg", [C, C]), sb("we", [C, EXPERTS, C])
    bg_rows, bout_rows = sb("bg_rows", [P, C]), sb("bout_rows", [P, C])
    be3 = sb("be3", [PARTS * EXPERTS, C], BF16)
    wT1 = sb("wT1", [P, 4, P])
    b1_nat, b1T, b2_sb = sb("b1_nat", [B * KC, P]), sb("b1T", [P, B * KC]), sb("b2_sb", [B, C])
    cT = sb("cT", [C, 2, B])
    modT = sb("modT", [C, 2, 4, B])
    gate_sb = sb("gate_sb", [B, 4, C])

    gates = [sb(f"gates{i}", [P, 4, C]) for i in range(3)]
    xs = [sb(f"x{i}", [P, T, C]) for i in range(4)]
    xn_f, hT_f = sb("xn_f", [P, T, C]), sb("hT_f", [C, N])
    st_f, mv_f, sm_f = sb("st_f", [P, T, 6]), sb("mv_f", [P, T, 2]), sb("sm_f", [P, 3, T])
    wv0b = sb("wv0b", [C, C])
    qk1_parts = [sb("q1_parts", [P, PARTS, N], BF16), sb("k1_parts", [P, PARTS, N], BF16)]
    qk0_parts = qk1_parts[0][0:2 * D0, :, :]
    rest = sb("rest", [P, N])
    q0_ops, k0_ops = qk1_parts[1][0:3 * D0, 0:2, :], sb("k0_ops", [3 * D0, 2, N], BF16)
    v0 = sb("v0", [P, T, C + 1])
    v0_later = sb("v0_later", [P, T - 1, C + 1])
    s0 = [sb(f"s0_{i}", [P, (T + 1) * P]) for i in range(2)]
    p0T = [sb(f"p0T{i}", [P, T + 1, P]) for i in range(2)]
    nm0, rs0 = sb("nm0", [P, T]), sb("rs0", [P, T])
    mx0 = sb("mx0", [P, T])
    top8, idx8 = sb("top8", [P, T, 8]), sb("idx8", [P, T, 8], U32)
    eidx, eidx_f = sb("eidx", [P, T], U32), sb("eidx_f", [P, T])
    ngmx, gsum, gp = sb("ngmx", [P, T]), sb("gsum", [P, T]), sb("gp", [P, T])
    onehot = sb("onehot", [P, T, PARTS, EXPERTS], BF16)
    onehotT = sb("onehotT", [PARTS * EXPERTS, N], BF16)
    hm = [sb(f"hm{i}", [C, EXPERTS, P]) for i in range(2)]
    q_ops = sb("q_ops", [P, SLOTS, GROUP, N], BF16)
    k_ops = sb("k_ops", [P, SLOTS, GROUP, N], BF16)
    v1 = [sb(f"v1_{i}", [P, T, HEADS, VW]) for i in range(2)]
    p_sb = [sb(f"p{i}", [P, N]) for i in range(4)]
    mx = [sb(f"row_max{i}", [P, 2 * T, HALVES]) for i in range(2)]
    nm = sb("nm", [P, 2 * T])
    nm_f, nm_r = sb("nm_f", [2 * T, P]), sb("nm_r", [2 * T, P])
    nm_parts = [sb(f"nm_parts{i}", [2 * T, PARTS, P], BF16) for i in range(2)]
    o_sb = sb("o_sb", [P, BANK])
    numer = sb("numer", [HEADS * DH, N])
    sums = sb("sums", [HEADS * T, P])
    over_sums = sb("over_sums", [HEADS * DH, N])
    xn_b = sb("xn_b", [P, T, C])
    hT_b = sb("hT_b", [C, N])
    st_b, mv_b, sm_b = sb("st_b", [P, T, 6]), sb("mv_b", [P, T, 2]), sb("sm_b", [P, 3, T])
    w1_sb, w2_sb = sb("w1_sb", [P, KC, C]), sb("w2_sb", [C, INTER])
    w2T = sb("w2T", [P, KC, C])
    wmod = [t[:, 0:6 * C].rearrange("p (j c) -> p j c", c=C) for t in (numer, over_sums)]
    w_nat = w1_sb
    gate_s = w2_sb[0:B, :].rearrange("p (j c) -> p j c", c=C)
    c_sb, c_e = (hT_b[0:B, i * 2 * C:(i + 1) * 2 * C].rearrange("p (l c) -> p l c", c=C) for i in range(2))
    wvd, wvu, wvdT = hT_b[:, 512:512 + D0], hT_b[0:D0, 640:640 + C], hT_b[0:D0, 768:768 + C]
    be_f, be_r = o_sb[0:EXPERTS, 0:C], o_sb[0:EXPERTS, C:2 * C]
    be_parts = o_sb[0:EXPERTS, 2 * C:2 * C + PARTS * C // 2].bitcast(BF16).rearrange("p (r c) -> p r c", c=C)
    wff = sb("wff", [C, 2, C])
    woutb, boutb = sb("woutb", [C, C]), sb("boutb", [P, C])
    parts_dram = nc.dram_tensor("parts", [2, 2, PARTS, P, N], BF16, kind="Internal").ap()
    attention_dram = nc.dram_tensor("attention", [2, HEADS, VW, N], F32, kind="Internal").ap()
    over_sums_dram = nc.dram_tensor("over_sums_rows", [HEADS, N], F32, kind="Internal").ap()

    def normalize(src, ready, xn, xn_free, st, mv, sm, on="pool"):
        small, marks = [], []
        halves = [slice(half * T // HALVES, (half + 1) * T // HALVES) for half in range(HALVES)]
        dve.wait(*ready)
        for tiles in halves:
            for t in range(tiles.start, tiles.stop):
                m = dve.do(lambda e, t=t: e.bn_stats(st[:, t, :], src[:, t, :]), "dve")
                if t % 2:
                    yield 0.25
            dve.wait(m)
            for t in range(tiles.start, tiles.stop):
                m = dve.do(lambda e, t=t: e.bn_aggr(mv[:, t, :], st[:, t, :]), "dve")
            pool.wait(m, mh_ready)
            pool.do(lambda e: e.tensor_scalar(sm[:, 0, tiles], mv[:, tiles, 0], -1.0, 0.0, ALU.mult, ALU.add), "pool")
            m = pool.do(lambda e: e.tensor_scalar(sm[:, 1, tiles], mv[:, tiles, 1], 1.0, EPS, ALU.mult, ALU.add), "pool")
            pool.wait(m)
            small.append(pool.do(lambda e: e.tensor_tensor(sm[:, 2, tiles], sm[:, 1, tiles], minus_half[:, tiles], op=ALU.pow), "pool"))
            yield 0.12
        for half, tiles in enumerate(halves):
            engines[on].wait(small[half], xn_free)
            for t in range(tiles.start, tiles.stop):
                m = engines[on].do(lambda e, t=t: e.tensor_scalar(
                    xn[:, t, :], src[:, t, :], sm[:, 0, t:t + 1], sm[:, 2, t:t + 1], ALU.add, ALU.mult), on)
            marks.append(m)
        for _ in range(EMPTY_AFTER["normalize"]):
            yield 0.4
        return marks

    def load(dst, src, signal="in_setup"):
        return sp.dma(dst, src, signal)

    x_loaded = {}

    def load_x(b, after=None):
        sp.wait(after)
        x_loaded[b] = sp.dma(xs[b % 4][:, :, :], x_in[b].rearrange("(t p) c -> p t c", p=P), f"in_x{b % 4}")

    load_x(0)
    for dst, src in ((c_sb[:, 0, :], c0), (c_sb[:, 1, :], c1), (const_sb[:, :], consts)):
        c_loaded = load(dst, src, "in_c")
    for dst, src in ((wmod[0][:, :, :], wmod0.rearrange("k (j c) -> k j c", c=C)),
                     (wmod[1][:, :, :], wmod1.rearrange("k (j c) -> k j c", c=C)),
                     (wvd[:, :], Wvdown), (wvu[:, :], Wvup)):
        loaded = load(dst, src)
    loaded_first = loaded
    for dst, src in ((wqk0[:, 0:D0], Wq0), (wqk0[:, D0:], Wk0), (sel[:, :, :], select.rearrange("k (b p) -> k b p", p=P)),
                     (wg[:, :], Wg), (bg_rows[:, :], bg.partition_broadcast(P)),
                     (we[:, :, :], We.rearrange("e c f -> c e f")), (be_f[:, :], be),
                     (w_nat[:, 0, :], Wq1), (w_nat[:, 1, :], Wk1), (w_nat[:, 2, :], Wv1), (w_nat[:, 3, :], Wout),
                     (bout_rows[:, :], bout.partition_broadcast(P)),
                     (b1_nat[:, :], b1.rearrange("g (k o) -> (g k) o", o=P)), (b2_sb[:, :], b2)):
        loaded_rest = load(dst, src, "in_rest")
    load_x(1)

    mh_ready = dve.do(lambda e: e.memset(minus_half[:, :], -0.5), "dve")
    v0_ones = dve.do(lambda e: e.memset(v0[:, :, C:C + 1], 1.0), "dve")
    first_norm = normalize(xs[0], [x_loaded[0]], xn_f, None, st_f, mv_f, sm_f, "dve")
    for _ in range(HALVES * (T // HALVES // 2 + 1)):
        next(first_norm)
    k_zero = pool.do(lambda e: e.memset(k_ops[:, :, :, :].bitcast(F32), 0.0), "pool")
    q_zero = pool.do(lambda e: e.memset(q_ops[:, :, :, :].bitcast(F32), 0.0), "pool")
    pool.wait(q_zero)
    k_ready = pool.do(lambda e: e.memset(k_ops[K_MAX:K_EXP, :, :, :].bitcast(F32), BF16_ONES), "pool")
    pool.wait(k_ready)

    act.wait(c_loaded)
    m = act.do(lambda e: e.activation(c_e[:, :, :], c_sb[:, :, :], ACT.Exp, scale=-1.0), "act")
    dve.wait(m)
    m = dve.do(lambda e: e.tensor_scalar(c_e[:, :, :], c_e[:, :, :], 1.0, None, ALU.add), "dve")
    dve.wait(m)
    m = dve.do(lambda e: e.reciprocal(c_e[:, :, :], c_e[:, :, :]), "dve")
    dve.wait(m)
    m = dve.do(lambda e: e.tensor_tensor(c_e[:, :, :], c_e[:, :, :], c_sb[:, :, :], op=ALU.mult), "dve")
    first_xn = finish(first_norm)
    ident_ready = dve.do(lambda e: e.tensor_copy(ident_bf[:, :], ident), "dve")
    bank = take()
    pe.wait(m, c_loaded)
    for j in range(2):
        m = pe.do(lambda e, j=j, v=bank.view: e.transpose(v[:, j * B:(j + 1) * B], c_e[:, j, :], ident[0:B, 0:B]), "pe")
    act.wait(m)
    cT_ready = bank.free = act.do(lambda e, v=bank.view: e.copy(cT[:, :, :], v[:, 0:2 * B].rearrange("p (l b) -> p l b", b=B)), "act")

    bank = take()
    pe.wait(cT_ready, loaded_first)
    mod_view = bank.view[:, 0:2 * 4 * B].rearrange("p (l j b) -> p l j b", l=2, j=4)
    for l in range(2):
        for j, six in enumerate((0, 1, 3, 4)):
            m = pe.do(lambda e, l=l, j=j, six=six, v=mod_view: e.matmul(
                v[:, l, j, :], wmod[l][:, six, :], cT[:, l, :], start=True, stop=True), "pe")
    dve.wait(m)
    dve.do(lambda e, v=mod_view: e.tensor_copy(modT[:, :, 0::2, :], v[:, :, 0::2, :]), "dve")
    mod_ready = bank.free = dve.do(lambda e, v=mod_view: e.tensor_scalar(
        modT[:, :, 1::2, :], v[:, :, 1::2, :], 1.0, None, ALU.add), "dve")

    bank = take()
    gate_view = bank.view[0:B, :].rearrange("p (j c) -> p j c", c=C)
    for l in range(2):
        for j, six in enumerate((2, 5)):
            m = pe.do(lambda e, l=l, j=j, six=six, v=gate_view: e.matmul(
                v[:, 2 * l + j, :], cT[:, l, :], wmod[l][:, six, :], start=True, stop=True), "pe")
    dve.wait(m)
    dve.do(lambda e, v=gate_view: e.tensor_scalar(gate_s, v, 0.0, 2.0, ALU.is_ge, ALU.mult), "dve")
    m = bank.free = dve.do(lambda e, v=gate_view: e.tensor_copy(gate_sb[:, :, :], v), "dve")
    flat, sign2 = gate_sb[:, :, :].rearrange("p j c -> p (j c)"), gate_s.rearrange("p j c -> p (j c)")
    dve.wait(m)
    m = dve.do(lambda e: e.scalar_tensor_tensor(flat, sign2, -1.0, flat, ALU.add, ALU.mult), "dve")
    dve.wait(m)
    m = dve.do(lambda e: e.tensor_scalar(flat, flat, 0.25, None, ALU.max), "dve")
    dve.wait(m)
    gate_ready = dve.do(lambda e: e.scalar_tensor_tensor(flat, sign2, -1.0, flat, ALU.add, ALU.mult), "dve")

    bank = take()
    m = pe.do(lambda e, v=bank.view: e.transpose(v[0:D0, 0:C], wvd[:, :], ident), "pe")
    act.wait(m)
    m = bank.free = act.do(lambda e, v=bank.view: e.copy(wvdT[:, :], v[0:D0, 0:C]), "act")
    bank = take()
    pe.wait(m)
    m = pe.do(lambda e, v=bank.view: e.matmul(v[:, 0:C], wvdT[:, :], wvu[:, :], start=True, stop=True), "pe")
    act.wait(m)
    wv0_ready = bank.free = act.do(lambda e, v=bank.view: e.copy(wv0[:, :], v[:, 0:C]), "act")
    act.wait(loaded_rest)
    wqk0_ready = act.do(lambda e: e.mul(wqk0[:, 0:D0], wqk0[:, 0:D0], D0 ** -0.5), "act")

    pe.wait(loaded_rest)
    bank = take()
    for j in range(4):
        m = pe.do(lambda e, j=j, v=bank.view: e.transpose(v[:, j * P:(j + 1) * P], w_nat[:, j, :], ident), "pe")
    act.wait(m)
    act.do(lambda e, v=bank.view: e.mul(wT1[:, 0:2, :], v[:, 0:2 * P].rearrange("p (j h) -> p j h", h=P), DH ** -0.25), "act")
    wT1_ready = bank.free = act.do(lambda e, v=bank.view: e.copy(
        wT1[:, 2:4, :], v[:, 2 * P:].rearrange("p (j h) -> p j h", h=P)), "act")
    bank = take()
    m = pe.do(lambda e, v=bank.view: e.transpose(v[:, 0:B * KC], b1_nat[:, :], ident[0:B * KC, 0:B * KC]), "pe")
    act.wait(m)
    b1T_ready = bank.free = act.do(lambda e, v=bank.view: e.copy(b1T[:, :], v[:, 0:B * KC]), "act")

    pv_bank.free = dve.do(lambda e: e.memset(pv_psum[:, :], 0.0), "dve")
    for v in v1:
        v1_ones = dve.do(lambda e, v=v: e.memset(v[:, :, :, DH:VW], 1.0), "dve")

    dve.wait(loaded_rest)
    m = dve.do(lambda e: e.tensor_copy(be_parts[:, 0, :], be_f[:, :]), "dve")
    dve.wait(m)
    m = dve.do(lambda e: e.tensor_tensor(be_r[:, :], be_f[:, :], be_parts[:, 0, :], op=ALU.subtract), "dve")
    dve.wait(m)
    m = dve.do(lambda e: e.tensor_copy(be_parts[:, 1, :], be_r[:, :]), "dve")
    dve.wait(m)
    m = dve.do(lambda e: e.tensor_tensor(be_parts[:, 2, :], be_r[:, :], be_parts[:, 1, :], op=ALU.subtract), "dve")
    sp.wait(m)
    for j in range(PARTS):
        be3_ready = sp.dma(be3[j * EXPERTS:(j + 1) * EXPERTS, :], be_parts[:, j, :], "be3")

    def to_channels(xn, xn_ready, hT, hT_free, block, which, b):
        pe.wait(mod_ready)
        for half in range(HALVES):
            pe.wait(xn_ready[half])
            bank = take()
            for j in range(4):
                m = pe.do(lambda e, t=4 * half + j, o=bank.view[:, j * P:(j + 1) * P]: e.transpose(
                    o, xn[:, t, :], ident), "pe" if j == 3 else None)
            act.wait(m, hT_free, mod_ready)
            r = bank.free = act.do(lambda e, half=half, v=bank.view: e.activation(
                hT[:, half * BANK:(half + 1) * BANK], v, ACT.Identity,
                scale=modT[:, block, which + 1, b:b + 1], bias=modT[:, block, which, b:b + 1]), "act")
            yield 0.3
        return r, m

    state = {"hT_f": None, "xn_f": None, "rest": None, "wv0b": None, "ops0": None, "v0": None, "s0": [None, None],
             "p0T": [None, None], "onehotT": None, "hm": [None, None], "parts1": [None, None],
             "hT_b": wv0_ready, "xn_b": None, "over_sums": None, "numer": None, "sums": None, "w12": None, "qk0": None,
             "parts_read": [None, None]}
    gates_ready, qkv_ready, v1_ready, x2_ready = {}, {}, {}, {}
    gates_done, v1_done = {-3: None, -2: None, -1: None}, {-2: None, -1: None}
    numer_done = {-2: None, -1: None}

    def split_parts(parts, r, ready, rows, on):
        q = engines[on]
        q.wait(ready)
        m = q.do(lambda e: e.tensor_tensor(r[0:rows, :], r[0:rows, :], parts[0:rows, 0, :], op=ALU.subtract), on)
        q.wait(m)
        m = q.do(lambda e: e.tensor_scalar(parts[0:rows, 1, :], r[0:rows, :], 1.0, 0.0, ALU.mult, ALU.add), on)
        q.wait(m)
        return q.do(lambda e: e.tensor_tensor(parts[0:rows, 2, :], r[0:rows, :], parts[0:rows, 1, :], op=ALU.subtract), on)

    def front(b):
        x, gate = xs[b % 4], gates[b % 3]
        on = "dve" if b == 0 else "pool"
        bank = take()
        pe.wait(gate_ready, loaded_rest)
        m = pe.do(lambda e, v=bank.view: e.matmul(v, sel[:, b, :], gate_sb[:, :, :].rearrange("p j c -> p (j c)"),
                                                  start=True, stop=True), "pe")
        act.wait(m, gates_done[b - 3])
        gates_ready[b] = bank.free = act.do(lambda e, v=bank.view: e.copy(gate[:, :, :].rearrange("p j c -> p (j c)"), v), "act")
        pool.wait(gates_ready[b], wv0_ready, state["wv0b"])
        wv0b_ready = pool.do(lambda e: e.tensor_tensor(wv0b[:, :], wv0[:, :], gate[:, 0, :], op=ALU.mult), "pool")
        yield 0.5

        xn_ready = first_xn if b == 0 else (
            yield from normalize(x, [x_loaded[b]], xn_f, state["xn_f"], st_f, mv_f, sm_f, on))
        hT_ready, state["xn_f"] = yield from to_channels(xn_f, xn_ready, hT_f, state["hT_f"], 0, 0, b)
        for half in range(HALVES):
            cols = slice(half * BANK, (half + 1) * BANK)
            bank = take()
            pe.wait(hT_ready, wqk0_ready)
            m = pe.do(lambda e, cols=cols, v=bank.view: e.matmul(v[0:2 * D0, :], wqk0[:, :], hT_f[:, cols], start=True, stop=True), "pe")
            act.wait(m, state["qk0"], state["parts1"][0])
            act.do(lambda e, cols=cols, v=bank.view: e.copy(qk0_parts[:, 0, cols], v[0:2 * D0, :]), "act")
            act.wait(state["rest"])
            m = bank.free = act.do(lambda e, cols=cols, v=bank.view: e.copy(rest[0:2 * D0, cols], v[0:2 * D0, :]), "act")
            yield 0.5
        m = state["rest"] = split_parts(qk0_parts, rest, m, 2 * D0, on)
        sp.wait(m, state["ops0"], state["parts1"][1])
        lo, hi = qk0_parts[0:D0, :, :], qk0_parts[D0:2 * D0, :, :]
        for dst, src in ((q0_ops[0:D0, :, :], lo[:, 0:2, :]), (q0_ops[D0:2 * D0, 0, :], lo[:, 1, :]),
                         (q0_ops[D0:2 * D0, 1, :], lo[:, 0, :]), (q0_ops[2 * D0:, :, :], lo[:, 0:3:2, :]),
                         (k0_ops[0:D0, :, :], hi[:, 0:2, :]), (k0_ops[D0:2 * D0, :, :], hi[:, 0:2, :]),
                         (k0_ops[2 * D0:, 0, :], hi[:, 2, :]), (k0_ops[2 * D0:, 1, :], hi[:, 0, :])):
            ops0_ready = state["qk0"] = sp.dma(dst, src, "first_block_ops")
        for _ in range(EMPTY_AFTER["first block's operands"]):
            yield 0.4
        for half in range(HALVES):
            bank = take()
            pe.wait(hT_ready, wv0b_ready)
            for j in range(4):
                t = 4 * half + j
                m = pe.do(lambda e, t=t, o=bank.view[:, j * C:(j + 1) * C]: e.matmul(
                    o, hT_f[:, t * P:(t + 1) * P], wv0b[:, :], start=True, stop=True), "pe" if j == 3 else None)
            act.wait(m, state["v0"])
            v0_ready = bank.free = act.do(lambda e, half=half, v=bank.view: e.copy(
                v0[:, 4 * half:4 * half + 4, 0:C], v.rearrange("p (t c) -> p t c", c=C)), "act")
            yield 0.5
        state["wv0b"] = state["hT_f"] = m
        pool.wait(v0_ready, v0_ones, state["v0"])
        m = pool.do(lambda e: e.tensor_scalar(v0_later[:, T - 2, :], v0[:, T - 1, :], 1.0, 0.0, ALU.mult, ALU.add), "pool")
        for i in range(T - 3, -1, -1):
            pool.wait(m)
            m = pool.do(lambda e, i=i: e.tensor_tensor(v0_later[:, i, :], v0_later[:, i + 1, :], v0[:, i + 1, :], op=ALU.add), "pool")
        later_ready = m
        yield 0.5

        s_ready, p_ready, pT_ready = {}, {}, {}

        def scores(i):
            s, n = s0[i % 2], (i + 1) * P
            pool.wait(state["s0"][i % 2])
            if i < T - 1:
                marks = [pool.do(lambda e: e.memset(s[:, 0:P], NEG), "pool")]
            else:
                marks = []
            for c in range(0, n, BANK):
                w = min(BANK, n - c)
                bank = take()
                pe.wait(ops0_ready)
                for half in range(2):
                    m = pe.do(lambda e, half=half, c=c, w=w, v=bank.view: e.matmul(
                        v[:, 0:w], q0_ops[:, half, i * P:(i + 1) * P], k0_ops[:, half, c:c + w],
                        start=half == 0, stop=half == 1), "pe" if half else None)
                state["ops0"] = m
                act.wait(m, state["s0"][i % 2])
                m = bank.free = act.do(lambda e, c=c, w=w, v=bank.view: e.copy(s[:, P + c:P + c + w], v[:, 0:w]), "act")
                yield 0.3
            pool.wait(m)
            marks.append(pool.do(lambda e: e.tensor_tensor(s[:, n:n + P], s[:, n:n + P], tril, op=ALU.mult), "pool"))
            s_ready[i] = marks

        def softmax(i):
            s, n = s0[i % 2], (i + 1) * P
            dve.wait(*s_ready[i], state["rest"])
            m = dve.do(lambda e: e.tensor_scalar(rest[:, 0:n], s[:, P:P + n], 0.0, NEG, ALU.is_equal, ALU.mult), "dve")
            if n > BANK:
                yield 0.3
            dve.wait(m)
            m = dve.do(lambda e: e.tensor_tensor_reduce(
                out=s[:, P:P + n], in0=s[:, P:P + n], in1=rest[:, 0:n], scale=1.0, scalar=NEG,
                op0=ALU.add, op1=ALU.max, accum_out=mx0[:, i:i + 1]), "dve")
            state["rest"] = m
            if n > BANK:
                yield 0.3
            dve.wait(m)
            m = dve.do(lambda e: e.tensor_scalar(nm0[:, i:i + 1], mx0[:, i:i + 1], -1.0, None, ALU.mult), "dve")
            first = P if i == T - 1 else 0
            act.wait(m, *s_ready[i])
            p_ready[i] = act.do(lambda e: e.activation(s[:, first:P + n], s[:, first:P + n], ACT.Exp, bias=nm0[:, i:i + 1]), "act")

        def transpose_p(i):
            s, pT = s0[i % 2], p0T[i % 2]
            blocks = list(range(1 if i == T - 1 else 0, i + 2))
            for c in range(0, len(blocks), 4):
                some = blocks[c:c + 4]
                bank = take()
                pe.wait(p_ready[i])
                for j, k in enumerate(some):
                    m = pe.do(lambda e, k=k, o=bank.view[:, j * P:(j + 1) * P]: e.transpose(
                        o, s[:, k * P:(k + 1) * P], ident), "pe" if k == some[-1] else None)
                dst, src = pT[:, some[0]:some[-1] + 1, :].rearrange("p k q -> p (k q)"), bank.view[:, 0:len(some) * P]
                act.wait(m, state["p0T"][i % 2])
                r = bank.free = act.do(lambda e, dst=dst, src=src: e.copy(dst, src), "act")
                pT_ready.setdefault(i, []).append(r)
                yield 0.3
            state["s0"][i % 2] = m

        def times_v(i):
            pT = p0T[i % 2]
            bank = take()
            pe.wait(*pT_ready[i], v0_ready, v0_ones, later_ready)
            o = bank.view[:, 0:C + 1]
            for k in range(i + 1):
                m = pe.do(lambda e, k=k: e.matmul(o, pT[:, k + 1, :], v0[:, k, :], start=k == 0, stop=i == T - 1 and k == i),
                          "pe" if i == T - 1 and k == i else None)
            if i < T - 1:
                m = pe.do(lambda e: e.matmul(o, pT[:, 0, :], v0_later[:, i, :], start=False, stop=True), "pe")
            state["p0T"][i % 2] = state["v0"] = m
            dve.wait(m)
            m = dve.do(lambda e: e.reciprocal(rs0[:, i:i + 1], o[:, C:C + 1]), "dve")
            dve.wait(m)
            bank.free = dve.do(lambda e: e.scalar_tensor_tensor(
                x[:, i, :], o[:, 0:C], rs0[:, i:i + 1], x[:, i, :], ALU.mult, ALU.add), "dve")
            yield 0.22 * (i + 2)
            return bank.free

        for n in range(T + 3):
            if n >= 3:
                x1_ready = yield from times_v(n - 3)
            if 2 <= n < T + 2:
                yield from transpose_p(n - 2)
            if 1 <= n < T + 1:
                yield from softmax(n - 1)
            if n < T:
                yield from scores(n)

        xn_ready = yield from normalize(x, [x1_ready], xn_f, state["xn_f"], st_f, mv_f, sm_f, on)
        hT_ready, state["xn_f"] = yield from to_channels(xn_f, xn_ready, hT_f, state["hT_f"], 0, 2, b)
        logits = xn_f
        for half in range(HALVES):
            bank = take()
            pe.wait(hT_ready, loaded_rest)
            for j in range(4):
                t = 4 * half + j
                m = pe.do(lambda e, t=t, o=bank.view[:, j * C:(j + 1) * C]: e.matmul(
                    o, hT_f[:, t * P:(t + 1) * P], wg[:, :], start=True, stop=True), "pe" if j == 3 else None)
            dve.wait(m, state["xn_f"], loaded_rest)
            lg = bank.free = dve.do(lambda e, half=half, v=bank.view: e.tensor_tensor(
                logits[:, 4 * half:4 * half + 4, :], v.rearrange("p (t c) -> p t c", c=C),
                bg_rows[:, :].unsqueeze(1).broadcast_to([P, 4, C]), op=ALU.add), "dve")
            yield 0.5
        dve.wait(lg)
        for t in range(T):
            m = dve.do(lambda e, t=t: e.max(top8[:, t, :], logits[:, t, :]), "dve")
            if t % 2:
                yield 0.25
        pool.wait(m)
        ng = pool.do(lambda e: e.tensor_scalar(ngmx[:, :], top8[:, :, 0], -1.0, 0.0, ALU.mult, ALU.add), "pool")
        dve.wait(m)
        for t in range(T):
            m = dve.do(lambda e, t=t: e.max_index(idx8[:, t, :], top8[:, t, :], logits[:, t, :]), "dve")
            if t % 2:
                yield 0.25
        dve.wait(m)
        em = dve.do(lambda e: e.tensor_scalar(eidx[:, :], idx8[:, :, 0], EXPERTS - 1, None, ALU.bitwise_and), "dve")
        dve.wait(em)
        em = dve.do(lambda e: e.tensor_copy(eidx_f[:, :], eidx[:, :]), "dve")
        dve.wait(em, state["onehotT"])
        oh_ready = dve.do(lambda e: e.tensor_tensor(
            onehot[:, :, :, :].rearrange("p t r e -> p t (r e)").rearrange("p t (r e) -> p t r e", r=PARTS),
            iota8.unsqueeze(1).unsqueeze(1).broadcast_to([P, T, PARTS, EXPERTS]),
            eidx_f[:, :].unsqueeze(2).unsqueeze(3).broadcast_to([P, T, PARTS, EXPERTS]), op=ALU.is_equal), "dve")
        act.wait(m, ng, lg)
        for t in range(T):
            m = act.do(lambda e, t=t: e.activation(logits[:, t, :], logits[:, t, :], ACT.Exp,
                                                   bias=ngmx[:, t:t + 1], accum_out=gsum[:, t:t + 1]), "act")
            if t % 4 == 3:
                yield 0.3
        yield 0.5
        dve.wait(m)
        exp_done = m
        gp_ready = dve.do(lambda e: e.reciprocal(gp[:, :], gsum[:, :]), "dve")
        yield 0.5
        bank = take()
        pe.wait(oh_ready, ident_ready)
        ohT = bank.view.bitcast(BF16)
        for t in range(T):
            m = pe.do(lambda e, t=t: e.transpose(ohT[0:PARTS * EXPERTS, t * P:(t + 1) * P],
                                                 onehot[:, t, :, :].rearrange("p r e -> p (r e)"), ident_bf[:, :]),
                      "pe" if t == T - 1 else None)
        act.wait(m, state["onehotT"])
        ohT_ready = bank.free = act.do(lambda e: e.copy(onehotT[:, :], ohT[0:PARTS * EXPERTS, :]), "act")
        yield 0.5
        picked = xn_f
        hm_ready = {}

        def mask(t):
            for quad in range(EXPERTS // 4):
                bank = take()
                for j in range(4):
                    m = pe.do(lambda e, k=4 * quad + j, o=bank.view[:, j * P:(j + 1) * P]: e.matmul(
                        o, onehot[:, t, 0, k:k + 1].broadcast_to([P, P]), ident_bf[:, :], start=True, stop=True),
                        "pe" if j == 3 else None)
                dve.wait(m, state["hm"][t % 2])
                hm_ready[t, quad] = bank.free = dve.do(lambda e, quad=quad, v=bank.view: e.tensor_tensor(
                    hm[t % 2][:, 4 * quad:4 * quad + 4, :], v.rearrange("p (k q) -> p k q", q=P),
                    hT_f[:, t * P:(t + 1) * P].unsqueeze(1).broadcast_to([C, 4, P]), op=ALU.mult), "dve")
                yield 0.35

        yield from mask(0)
        for t in range(T):
            if t < T - 1:
                yield from mask(t + 1)
            bank = take()
            o = bank.view[:, 0:C]
            pe.wait(ohT_ready, be3_ready)
            pe.do(lambda e, t=t: e.matmul(o, onehotT[:, t * P:(t + 1) * P], be3[:, :], start=True, stop=False))
            for k in range(EXPERTS):
                pe.wait(hm_ready[t, k // 4])
                m = pe.do(lambda e, k=k, t=t: e.matmul(o, hm[t % 2][:, k, :], we[:, k, :], start=False, stop=k == EXPERTS - 1),
                          "pe" if k == EXPERTS - 1 else None)
            state["hm"][t % 2] = m
            act.wait(m, gp_ready, exp_done)
            r = bank.free = act.do(lambda e, t=t: e.activation(picked[:, t, :], o, ACT.Relu, scale=gp[:, t:t + 1]), "act")
            yield 1.0
            if t % 4 == 3:
                tiles = slice(t - 3, t + 1)
                pool.wait(r)
                g = pool.do(lambda e, tiles=tiles: e.tensor_tensor(
                    picked[:, tiles, :], picked[:, tiles, :], gate[:, 1, :].unsqueeze(1).broadcast_to([P, 4, C]), op=ALU.mult), "pool")
                pool.wait(g)
                x2 = pool.do(lambda e, tiles=tiles: e.tensor_tensor(x[:, tiles, :], x[:, tiles, :], picked[:, tiles, :], op=ALU.add), "pool")
        state["hT_f"] = state["onehotT"] = m
        state["xn_f"] = x2
        yield 0.5

        xn_ready = yield from normalize(x, [x2], xn_f, state["xn_f"], st_f, mv_f, sm_f, on)
        x2_ready[b] = xn_ready[-1]
        hT_ready, state["xn_f"] = yield from to_channels(xn_f, xn_ready, hT_f, state["hT_f"], 1, 0, b)
        rests = (rest, xn_f[:, :, :].rearrange("p t c -> p (t c)"))
        for w, parts in enumerate(qk1_parts):
            r = rests[w]
            for half in range(HALVES):
                cols = slice(half * BANK, (half + 1) * BANK)
                bank = take()
                pe.wait(hT_ready, wT1_ready)
                m = pe.do(lambda e, w=w, cols=cols, v=bank.view: e.matmul(v, wT1[:, w, :], hT_f[:, cols], start=True, stop=True), "pe")
                act.wait(m, state["parts1"][w], state["ops0"] if w else state["qk0"])
                act.do(lambda e, cols=cols, v=bank.view, parts=parts: e.copy(parts[:, 0, cols], v), "act")
                act.wait(state["rest"] if w == 0 else state["xn_f"])
                m = bank.free = act.do(lambda e, cols=cols, v=bank.view, r=r: e.copy(r[:, cols], v), "act")
                yield 0.5
            m = split_parts(parts, r, m, P, on)
            if w == 0:
                state["rest"] = m
            else:
                state["xn_f"] = m
            sp.wait(m, state["parts_read"][b % 2])
            state["parts1"][w] = sp.dma(parts_dram[b % 2, w].rearrange("r p n -> p r n"), parts[:, :, :], f"parts{w}")
        qkv_ready[b] = list(state["parts1"])
        for half in range(HALVES):
            bank = take()
            for j in range(4):
                t = 4 * half + j
                m = pe.do(lambda e, t=t, o=bank.view[:, j * P:(j + 1) * P]: e.matmul(
                    o, hT_f[:, t * P:(t + 1) * P], wT1[:, 2, :], start=True, stop=True), "pe" if j == 3 else None)
            act.wait(m, v1_done[b - 2])
            v1_ready[b] = bank.free = act.do(lambda e, half=half, v=bank.view: e.copy(
                v1[b % 2][:, 4 * half:4 * half + 4, :, 0:DH], v.rearrange("p (t h d) -> p t h d", t=4, d=DH)), "act")
            yield 0.5
        state["hT_f"] = m

    slot_free, ops_ready, m_ready = [None] * SLOTS, {}, {}

    def load_operands(g):
        b, slot, h0 = g // GROUPS, g % SLOTS, (g % GROUPS) * GROUP
        sp.wait(slot_free[slot], q_zero, k_ready)
        for w, (ops, which) in enumerate(((q_ops, Q_PART), (k_ops, K_PART))):
            sp.wait(qkv_ready[b][w])
            for r, part in enumerate(which):
                src = parts_dram[b % 2, w, part, h0 * DH:(h0 + GROUP) * DH, :].rearrange("(h d) n -> d h n", d=DH)
                ops_ready[g] = sp.dma(ops[r * DH:(r + 1) * DH, slot, :, :], src, f"operands{slot}")
        state["parts_read"][b % 2] = ops_ready[g]

    mx_free = [None, None]
    mx_ready = {}

    def maxima(pair):
        g = pair // 2
        slot = g % SLOTS
        for hh in range(2):
            h = 2 * (pair % 2) + hh
            for i in range(T):
                for half in range(HALVES):
                    bank = take()
                    pe.wait(ops_ready[g])
                    m = pe.do(lambda e, h=h, i=i, half=half, v=bank.view: e.matmul(
                        v, q_ops[0:K_MAX, slot, h, i * P:(i + 1) * P], k_ops[0:K_MAX, slot, h, half * BANK:(half + 1) * BANK],
                        start=True, stop=True), "pe_max")
                    dve.wait(m, mx_free[pair % 2])
                    bank.free = mx_ready[pair] = dve.do(lambda e, hh=hh, i=i, half=half, v=bank.view: e.tensor_reduce(
                        mx[pair % 2][:, hh * T + i, half:half + 1], v, axis=AX.X, op=ALU.max), "dve")
                    yield 0.5

    nm_parts_free = [None, None]
    nm_free = [None, None]

    def subtract_maxima(pair):
        buf, slot, h0 = pair % 2, pair // 2 % SLOTS, 2 * (pair % 2)
        parts = nm_parts[buf]
        dve.wait(mx_ready[pair], nm_free[0])
        mx_free[buf] = m = dve.do(lambda e: e.tensor_reduce(nm[:, :], mx[buf][:, :, :], axis=AX.X, op=ALU.max, negate=True), "dve")
        yield 0.5
        bank = take()
        v = bank.view[0:2 * T, 0:P]
        pe.wait(m)
        nm_free[0] = m = pe.do(lambda e: e.transpose(v, nm[:, :], ident), "pe")
        act.wait(m, nm_parts_free[buf], nm_free[1])
        hi = act.do(lambda e: e.copy(parts[:, 0, :], v), "act")
        bank.free = m = act.do(lambda e: e.copy(nm_f[:, :], v), "act")
        yield 0.5
        pool.wait(m, hi)
        m = pool.do(lambda e: e.tensor_tensor(nm_r[:, :], nm_f[:, :], parts[:, 0, :], op=ALU.subtract), "pool")
        pool.wait(m)
        m = pool.do(lambda e: e.tensor_scalar(parts[:, 1, :], nm_r[:, :], 1.0, 0.0, ALU.mult, ALU.add), "pool")
        pool.wait(m)
        nm_free[1] = m = pool.do(lambda e: e.tensor_tensor(parts[:, 2, :], nm_r[:, :], parts[:, 1, :], op=ALU.subtract), "pool")
        sp.wait(m)
        for j in range(PARTS):
            dst = q_ops[K_MAX + j:K_MAX + j + 1, slot, h0:h0 + 2, :].rearrange("o h (i q) -> o (h i) q", q=P)
            m_ready[pair] = nm_parts_free[buf] = sp.dma(dst, parts[:, j, :], f"maxima{buf}")
        yield 0.5

    p_free = [None] * 4
    o_free = [be3_ready]
    out_ready = {}
    exps = {}

    def score_step(step, hh):
        pair, kb = divmod(step, T)
        g = pair // 2
        slot, h = g % SLOTS, 2 * (pair % 2) + hh
        buf = (2 * step + hh) % 4
        for half in range(HALVES):
            bank, cols = take(), slice(half * BANK, (half + 1) * BANK)
            pe.wait(m_ready[pair])
            m = pe.do(lambda e, v=bank.view, cols=cols: e.matmul(
                v, k_ops[0:K_EXP, slot, h, kb * P:(kb + 1) * P], q_ops[0:K_EXP, slot, h, cols], start=True, stop=True), "pe_scores")
            act.wait(m, p_free[buf])
            bank.free = exps[step, hh] = act.do(
                lambda e, v=bank.view, cols=cols: e.activation(p_sb[buf][:, cols], v, ACT.Exp), "act_exp")
        if kb == T - 1 and pair % 2 and hh:
            slot_free[slot] = m

    def value_step(step):
        pair, kb = divmod(step, T)
        b, hp = divmod(pair, HEADS // 2)
        v = v1[b % 2]
        if kb == 0:
            pe.wait(pv_bank.free, v1_ready[b], v1_ones)
        pe.wait(exps[step, 0], exps[step, 1])
        for hh in range(2):
            buf = (2 * step + hh) % 4
            for half in range(HALVES):
                q = 32 * (2 * hh + half)
                m = pe.do(lambda e, hh=hh, half=half, q=q, buf=buf: e.matmul(
                    pv_psum[q:q + VW, :], v[:, kb, 2 * hp + hh, :], p_sb[buf][:, half * BANK:(half + 1) * BANK],
                    start=kb == 0, stop=kb == T - 1), "pe_pv" if half else None)
            p_free[buf] = m
        if kb < T - 1:
            return
        if hp == HEADS // 2 - 1:
            v1_done[b] = m
        act.wait(m, o_free[0])
        pv_bank.free = m = act.do(lambda e: e.copy(o_sb[:, :], pv_psum[:, :]), "act")
        sp.wait(m, numer_done[b - 2])
        for hh in range(2):
            for half in range(HALVES):
                q = 32 * (2 * hh + half)
                o_free[0] = out_ready[b] = sp.dma(attention_dram[b % 2, 2 * hp + hh, :, half * BANK:(half + 1) * BANK], o_sb[q:q + VW, :], "attention_out")

    stored, weights = {}, {}

    def back_weights(b):
        gate = gates[b % 3]
        sp.wait(state["w12"], wT1_ready, gate_ready)
        sp.dma(w1_sb[:, :, :], W1[b].rearrange("(k o) c -> o k c", o=P), "in_w12")
        w12 = sp.dma(w2_sb[:, :], W2[b], "in_w12")
        for _ in range(3):
            yield 0.5
        pool.wait(gates_ready[b], wT1_ready, state["woutb"])
        pool.do(lambda e: e.tensor_tensor(woutb[:, :], wT1[:, 3, :], gate[:, 2, :], op=ALU.mult), "pool")
        wb = pool.do(lambda e: e.tensor_tensor(boutb[:, :], bout_rows[:, :], gate[:, 2, :], op=ALU.mult), "pool")
        yield 0.5
        bank = take()
        pe.wait(w12)
        for j in range(KC):
            m = pe.do(lambda e, j=j, o=bank.view[:, j * P:(j + 1) * P]: e.transpose(o, w2_sb[:, j * P:(j + 1) * P], ident),
                      "pe" if j == KC - 1 else None)
        act.wait(m, state["w12"])
        m = bank.free = act.do(lambda e, v=bank.view: e.copy(w2T[:, :, :].rearrange("p k c -> p (k c)"), v), "act")
        yield 0.5
        bank = take()
        pe.wait(m, b1T_ready)
        v = bank.view[:, 0:2 * C]
        for j in range(KC):
            pe.do(lambda e, j=j: e.matmul(v[:, 0:C], w1_sb[:, j, :], w2T[:, j, :], start=j == 0, stop=j == KC - 1))
        for j in range(KC):
            col = b1T[:, b * KC + j:b * KC + j + 1].broadcast_to([P, P])
            pe.do(lambda e, j=j, col=col: e.matmul(v[:, C:2 * C], col, w2T[:, j, :], start=j == 0, stop=False))
        state["w12"] = m = pe.do(lambda e: e.matmul(v[:, C:2 * C], sel[:, b, :], b2_sb[:, :], start=False, stop=True), "pe")
        dve.wait(m, gates_ready[b], state["wff"])
        wff_ready = bank.free = dve.do(lambda e: e.tensor_tensor(
            wff[:, :, :], v.rearrange("p (j c) -> p j c", c=C), gate[:, 3, :].unsqueeze(1).broadcast_to([P, 2, C]), op=ALU.mult), "dve")
        gates_done[b] = wff_ready
        yield 0.5
        x = xs[b % 4]
        pool.wait(wb, x2_ready[b])
        xb = pool.do(lambda e: e.tensor_tensor(x[:, :, :], x[:, :, :], rows(boutb[:, :]), op=ALU.add), "pool")
        weights[b] = wb, wff_ready, xb
        yield 0.5

    def rows(tile):
        return tile.unsqueeze(1).broadcast_to([P, T, C])

    def back(b):
        x = xs[b % 4]
        on = "dve" if b == B - 1 else "pool"
        for _ in range(3):
            yield 0.5
        sp.wait(out_ready[b], state["numer"], state["sums"], gate_ready)
        m = sp.dma(sums[:, :], attention_dram[b % 2, :, DH, :].rearrange("h (i q) -> h i q", q=P), "sums_in")
        numer_ready = numer_done[b] = sp.dma(numer[:, :], attention_dram[b % 2, :, 0:DH, :], "numer_in")
        for _ in range(2):
            yield 0.5
        dve.wait(m)
        m = dve.do(lambda e: e.reciprocal(sums[:, :], sums[:, :]), "dve")
        sp.wait(m)
        m = state["sums"] = sp.dma(over_sums_dram.rearrange("h (i q) -> (h i) q", q=P), sums[:, :], "over_sums_out")
        yield 0.5
        sp.wait(m, state["over_sums"])
        spread = sp.dma(over_sums[:, :], over_sums_dram.unsqueeze(1).broadcast_to([HEADS, DH, N]), "over_sums_in")
        for _ in range(EMPTY_AFTER["sums"]):
            yield 0.5
        wb, wff_ready, xb = weights[b]
        a = numer
        for half in range(HALVES):
            cols = slice(half * BANK, (half + 1) * BANK)
            engines[on].wait(numer_ready, spread)
            aT_ready = engines[on].do(lambda e, cols=cols: e.tensor_tensor(
                a[:, cols], a[:, cols], over_sums[:, cols], op=ALU.mult), on)
        for _ in range(EMPTY_AFTER["numerators"]):
            yield 0.5
        for half in range(HALVES):
            bank = take()
            pe.wait(aT_ready, wb)
            for j in range(4):
                t = 4 * half + j
                m = pe.do(lambda e, t=t, o=bank.view[:, j * C:(j + 1) * C]: e.matmul(
                    o, a[:, t * P:(t + 1) * P], woutb[:, :], start=True, stop=True), "pe" if j == 3 else None)
            dve.wait(m, xb)
            x3 = bank.free = dve.do(lambda e, half=half, v=bank.view: e.tensor_tensor(
                x[:, 4 * half:4 * half + 4, :], v.rearrange("p (t c) -> p t c", c=C), x[:, 4 * half:4 * half + 4, :], op=ALU.add), "dve")
            yield 0.5
        state["numer"] = state["woutb"] = m
        state["over_sums"] = aT_ready
        xn_ready = yield from normalize(x, [x3], xn_b, state["xn_b"], st_b, mv_b, sm_b, on)
        pool.wait(wff_ready, xn_ready[-1])
        xb = pool.do(lambda e: e.tensor_tensor(x[:, :, :], x[:, :, :], rows(wff[:, 1, :]), op=ALU.add), "pool")
        hT_ready, state["xn_b"] = yield from to_channels(xn_b, xn_ready, hT_b, state["hT_b"], 1, 2, b)
        for half in range(HALVES):
            bank = take()
            pe.wait(hT_ready, wff_ready)
            for j in range(4):
                t = 4 * half + j
                m = pe.do(lambda e, t=t, o=bank.view[:, j * C:(j + 1) * C]: e.matmul(
                    o, hT_b[:, t * P:(t + 1) * P], wff[:, 0, :], start=True, stop=True), "pe" if j == 3 else None)
            dve.wait(m, xb)
            y = bank.free = dve.do(lambda e, half=half, v=bank.view: e.tensor_tensor(
                x[:, 4 * half:4 * half + 4, :], v.rearrange("p (t c) -> p t c", c=C), x[:, 4 * half:4 * half + 4, :], op=ALU.add), "dve")
            yield 0.5
            tiles = slice(4 * half, 4 * half + 4)
            sp.wait(y)
            stored[b] = sp.dma(out[b].rearrange("(t p) c -> p t c", p=P)[:, tiles, :], x[:, tiles, :], f"out{b % 2}")
        state["hT_b"] = state["wff"] = m
    state["woutb"] = state["wff"] = None

    finish(front(0))
    load_x(2)

    done, now = {"front": 0}, [0]
    FRONT_FROM = -T - LEAD

    def fronts():
        for b in range(1, B):
            while now[0] < FRONT_FROM + (b - 1) * T * HEADS // 2:
                yield 1.0
            yield from front(b)
            done["front"] = b

    def backs(b):
        yield from back(b)
        if b + 4 < B:
            load_x(b + 4, stored[b])

    beside = []
    PAIRS = B * HEADS // 2

    def advance(share):
        for job in list(beside):
            job[2] += job[1] * share * (LEAD_IN_RATE if now[0] < 0 else 1)
            while job[2] > 0:
                cost = next(job[0], None)
                if cost is None:
                    beside.remove(job)
                    break
                job[2] -= cost

    fronts_job = [fronts(), FRONT_COST / (T * HEADS // 2), 0.0]
    beside.append(fronts_job)
    load_x(3)
    max_steps = None
    for step in range(-LEAD, PAIRS * T + 1):
        now[0] = step
        lead, lead_kb = divmod(step + LEAD, T)
        if lead_kb == 0 and lead < PAIRS:
            for g in ((0, 1) if lead == 0 else (lead // 2 + 1,) if lead % 2 and lead > 1 else ()):
                if g < B * GROUPS:
                    while done["front"] < g // GROUPS:
                        next(fronts_job[0], None)
                    load_operands(g)
            max_steps = maxima(lead)
        for n in range(4):
            if lead < PAIRS:
                next(max_steps, None)
            if n < 2 and 0 <= step < PAIRS * T:
                score_step(step, n)
            if n == 2 and step > 0:
                value_step(step - 1)
            advance(SHARES[n])
        if lead < PAIRS and lead_kb == T - 1:
            next(max_steps, None)
            beside.append([subtract_maxima(lead), BACK_RATE, 0.0])
        if step > 0 and step % (T * HEADS // 2) == BACK_WEIGHTS_STEP:
            beside.append([back_weights(step // (T * HEADS // 2)), BACK_RATE / 2, 0.0])
        if step > 0 and step % (T * HEADS // 2) == 0:
            b = step // (T * HEADS // 2) - 1
            beside.append([backs(b), BACK_RATE, 0.0])
    for job in list(beside):
        finish(job[0])

    sp.wait(*stored.values(), *state["parts1"])


NAMES = ["L0_attn_inputs", "L0_attn_Wq", "L0_attn_Wk", "L0_attn_Wvdown", "L0_attn_Wvup", "L0_ffn_Wg", "L0_ffn_bg",
         "L0_ffn_We", "L0_ffn_be", "L0_c", "L0_wmod", "L1_attn_Wq", "L1_attn_Wk", "L1_attn_Wv", "L1_attn_Wout",
         "L1_attn_bout", "L1_ffn_W1", "L1_ffn_b1", "L1_ffn_W2", "L1_ffn_b2", "L1_c", "L1_wmod"]


def kernel(**inputs):
    from contextlib import ExitStack
    import concourse.bacc as bacc
    from concourse.bass_utils import run_bass_kernel_spmd

    nc = bacc.Bacc("TRN2", target_bir_lowering=False, num_devices=1)
    arrays = {name: np.ascontiguousarray(inputs[name]) for name in NAMES}
    iota = np.broadcast_to(np.arange(EXPERTS, dtype=np.float32), (P, EXPERTS))
    arrays["consts"] = np.concatenate([np.eye(P, dtype=np.float32), np.tril(np.ones((P, P), np.float32)), iota], axis=1)
    arrays["select"] = np.repeat(np.eye(B, dtype=np.float32), P, axis=1)
    args = [nc.dram_tensor(f"in_{n}", a.shape, mybir.dt.from_np(a.dtype), kind="ExternalInput").ap() for n, a in arrays.items()]
    out = nc.dram_tensor("out", (B, N, C), F32, kind="ExternalOutput").ap()
    with ExitStack() as ctx:
        build(nc, ctx, *args, out)
    result = run_bass_kernel_spmd(nc, [{f"in_{n}": a for n, a in arrays.items()}], core_ids=[0])
    return result.results[0]["out"]
```
